# Optimizing a Trainium2 kernel written in Bass

```python
import numpy as np
import jax
import jax.numpy as jnp

def _softmax(x, axis=-1):
    return jax.nn.softmax(x, axis=axis)

def _gelu(x):
    return jax.nn.gelu(x, approximate=True)

def _silu(x):
    return jax.nn.silu(x)

def _sigmoid(x):
    return jax.nn.sigmoid(x)

def _layernorm(x, axis=-1, eps=1e-05):
    m = jnp.mean(x, axis=axis, keepdims=True)
    v = jnp.var(x, axis=axis, keepdims=True)
    return (x - m) / jnp.sqrt(v + eps)

def _scatter_add(tgt, idx, src, axis=0):
    return tgt.at[idx].add(src)

def _segment_sum(src, seg, n):
    return jax.ops.segment_sum(src, seg, n)
kernel_name = 'mk_perceiver_d1_seqx_r2_4ba89f'

def setup_inputs(seed: int=0):
    np.random.seed(seed)
    _w = jnp.asarray

    def _rec_inputs():
        import jax
        import jax.numpy as jnp
        _rk = jax.random.key(seed)
        x = -0.000125 + 0.9999 * jax.random.normal(jax.random.fold_in(_rk, 1), (2, 512, 512), jnp.float32)
        _lenS = 512 - jax.random.randint(jax.random.fold_in(_rk, 7), (2,), 0, max(1, 512 // 4) + 1, jnp.int32)
        _lenS2 = 8192 - jax.random.randint(jax.random.fold_in(_rk, 8), (2,), 0, max(1, 8192 // 4) + 1, jnp.int32)
        _ctx_1024P = jax.random.normal(jax.random.fold_in(_rk, 11), (2, 16, 512), jnp.float32)
        _ctx_1024c = jax.random.dirichlet(jax.random.fold_in(_rk, 511), 0.3 * jnp.ones((16,), jnp.float32), (2, 8192))
        _ctx_1024t = jnp.einsum('bsk,bkd->bsd', _ctx_1024c, _ctx_1024P)
        _ctx_1024t = _ctx_1024t * jax.lax.rsqrt(jnp.mean(jnp.square(_ctx_1024t)) + 1e-12) * 0.953939
        ctx_1024 = -1.78809e-06 + 0.0312453 * (_ctx_1024t + 0.3 * jax.random.normal(jax.random.fold_in(_rk, 611), (2, 8192, 512), jnp.float32))
        return (x, ctx_1024)
    x, ctx_1024 = _rec_inputs()

    def _L0_xattn_setup():
        import jax, jax.numpy as jnp
        import numpy as np
        E, T, H, F = (16, 1024, 512, 2048)
        key = jax.random.key(seed)
        kx, k1, k2, k3 = jax.random.split(key, 4)
        s = 1.0 / np.sqrt(H)
        return {'x': jax.random.normal(kx, (E, T, H), dtype=jnp.float32), 'w1': jax.random.normal(k1, (E, F, H), dtype=jnp.float32) * s, 'v1': jax.random.normal(k2, (E, F, H), dtype=jnp.float32) * s, 'w2': jax.random.normal(k3, (E, F, H), dtype=jnp.float32) * s}
    _L0_xattn_all = _L0_xattn_setup()
    _L0_xattn_in = {k: v for k, v in _L0_xattn_all.items() if k in ()}
    del _L0_xattn_all

    def _L0_attn_setup():
        import jax, jax.numpy as jnp
        import numpy as np
        DIM = 512
        DIM_HEAD = 64
        HEADS = 8
        INNER = DIM_HEAD * HEADS
        SCALE = DIM_HEAD ** (-0.5)
        COS_SCALE = 1.0

        def layer_norm(x, w, b, eps=1e-05):
            mu = jnp.mean(x, axis=-1, keepdims=True)
            var = jnp.var(x, axis=-1, keepdims=True)
            return (x - mu) * jax.lax.rsqrt(var + eps) * w + b
        key = jax.random.key(seed)
        ks = jax.random.split(key, 6)
        x = jax.random.normal(ks[0], (4, 1024, DIM), dtype=jnp.float32)
        Wq = jax.random.normal(ks[1], (DIM, INNER), dtype=jnp.float32) * DIM ** (-0.5)
        Wkv = jax.random.normal(ks[2], (DIM, 2 * DIM_HEAD), dtype=jnp.float32) * DIM ** (-0.5)
        Wo = jax.random.normal(ks[3], (INNER, DIM), dtype=jnp.float32) * INNER ** (-0.5)
        norm_w = jnp.ones((DIM,), jnp.float32)
        norm_b = jnp.zeros((DIM,), jnp.float32)
        out_norm_w = jnp.ones((DIM,), jnp.float32)
        out_norm_b = jnp.zeros((DIM,), jnp.float32)
        return {'x': x, 'Wq': Wq, 'Wkv': Wkv, 'Wo': Wo, 'norm_w': norm_w, 'norm_b': norm_b, 'out_norm_w': out_norm_w, 'out_norm_b': out_norm_b}
    _L0_attn_all = _L0_attn_setup()
    _L0_attn_in = {k: v for k, v in _L0_attn_all.items() if k in ('Wq', 'Wkv', 'Wo', 'norm_w', 'norm_b', 'out_norm_w', 'out_norm_b')}
    del _L0_attn_all

    def _L0_ffn_setup():
        import jax, jax.numpy as jnp
        import numpy as np
        JITTER_EPS = 0.01
        NEG_INF = -jnp.inf

        def sparsemixer_eval(scores, jitter_eps):
            m1 = jnp.max(scores, axis=-1, keepdims=True)
            ind1 = jnp.argmax(scores, axis=-1)
            factor1 = jnp.maximum(jnp.abs(scores), m1)
            mask1 = jax.lax.stop_gradient((m1 - scores) / factor1 > 2.0 * jitter_eps)
            gates1 = jax.nn.softmax(jnp.where(mask1, NEG_INF, scores), axis=-1)
            mult1 = jnp.take_along_axis(gates1, ind1[:, None], axis=-1)[:, 0]
            E = scores.shape[-1]
            onehot1 = ind1[:, None] == jnp.arange(E)[None, :]
            masked_scores = jnp.where(onehot1, NEG_INF, scores)
            m2 = jnp.max(masked_scores, axis=-1, keepdims=True)
            ind2 = jnp.argmax(masked_scores, axis=-1)
            factor2 = jnp.maximum(jnp.abs(scores), m2)
            mask2 = jax.lax.stop_gradient((m2 - scores) / factor2 > 2.0 * jitter_eps)
            gates2 = jax.nn.softmax(jnp.where(mask2, NEG_INF, masked_scores), axis=-1)
            mult2 = jnp.take_along_axis(gates2, ind2[:, None], axis=-1)[:, 0]
            multiplier = jnp.stack([mult1, mult2], axis=-1)
            selected = jnp.stack([ind1, ind2], axis=-1)
            return (multiplier, selected)
        key = jax.random.key(seed)
        k0, k1, k2, k3, k4 = jax.random.split(key, 5)
        B, S, H, F, E = (2, 512, 512, 1024, 8)
        scale = 0.02
        return {'hidden_states': jax.random.normal(k0, (B, S, H), dtype=jnp.float32), 'router_w': jax.random.normal(k1, (E, H), dtype=jnp.float32) * scale, 'w_gate': jax.random.normal(k2, (E, F, H), dtype=jnp.float32) * scale, 'w_up': jax.random.normal(k3, (E, F, H), dtype=jnp.float32) * scale, 'w_down': jax.random.normal(k4, (E, H, F), dtype=jnp.float32) * scale}
    _L0_ffn_all = _L0_ffn_setup()
    _L0_ffn_in = {k: v for k, v in _L0_ffn_all.items() if k in ('router_w', 'w_gate', 'w_up', 'w_down')}
    del _L0_ffn_all
    return {'x': x, 'ctx_1024': ctx_1024, 'L0_attn_Wq': _L0_attn_in['Wq'], 'L0_attn_Wkv': _L0_attn_in['Wkv'], 'L0_attn_Wo': _L0_attn_in['Wo'], 'L0_attn_norm_w': _L0_attn_in['norm_w'], 'L0_attn_norm_b': _L0_attn_in['norm_b'], 'L0_attn_out_norm_w': _L0_attn_in['out_norm_w'], 'L0_attn_out_norm_b': _L0_attn_in['out_norm_b'], 'L0_ffn_router_w': _L0_ffn_in['router_w'], 'L0_ffn_w_gate': _L0_ffn_in['w_gate'], 'L0_ffn_w_up': _L0_ffn_in['w_up'], 'L0_ffn_w_down': _L0_ffn_in['w_down']}

def reference(x, ctx_1024, L0_attn_Wq, L0_attn_Wkv, L0_attn_Wo, L0_attn_norm_w, L0_attn_norm_b, L0_attn_out_norm_w, L0_attn_out_norm_b, L0_ffn_router_w, L0_ffn_w_gate, L0_ffn_w_up, L0_ffn_w_down):
    import jax
    import jax.numpy as jnp

    def _L0_xattn_ref(x, w1, v1, w2):
        import jax, jax.numpy as jnp
        import numpy as np
        E, T, H, F = (16, 1024, 512, 2048)
        x1 = jnp.einsum('eth,efh->etf', x, w1)
        x2 = jnp.einsum('eth,efh->etf', x, v1)
        h = jax.nn.gelu(x1, approximate=True) * x2
        return jnp.einsum('etf,efh->eth', h, w2)

    def _L0_attn_ref(x, Wq, Wkv, Wo, norm_w, norm_b, out_norm_w, out_norm_b):
        import jax, jax.numpy as jnp
        import numpy as np
        DIM = 512
        DIM_HEAD = 64
        HEADS = 8
        INNER = DIM_HEAD * HEADS
        SCALE = DIM_HEAD ** (-0.5)
        COS_SCALE = 1.0

        def layer_norm(x, w, b, eps=1e-05):
            mu = jnp.mean(x, axis=-1, keepdims=True)
            var = jnp.var(x, axis=-1, keepdims=True)
            return (x - mu) * jax.lax.rsqrt(var + eps) * w + b
        b, n, _ = x.shape
        xn = layer_norm(x, norm_w, norm_b)
        q = xn @ Wq
        kv = xn @ Wkv
        k, v = (kv[..., :DIM_HEAD], kv[..., DIM_HEAD:])
        q = q.reshape(b, n, HEADS, DIM_HEAD).transpose(0, 2, 1, 3) * SCALE
        sim = jnp.einsum('bhid,bjd->bhij', q, k) * COS_SCALE
        attn = jax.nn.softmax(sim.astype(jnp.float32), axis=-1).astype(sim.dtype)
        out = jnp.einsum('bhij,bjd->bhid', attn, v)
        out = out.transpose(0, 2, 1, 3).reshape(b, n, INNER)
        out = out @ Wo
        return layer_norm(out, out_norm_w, out_norm_b)

    def _L0_ffn_ref(hidden_states, router_w, w_gate, w_up, w_down):
        import jax, jax.numpy as jnp
        import numpy as np
        JITTER_EPS = 0.01
        NEG_INF = -jnp.inf

        def sparsemixer_eval(scores, jitter_eps):
            m1 = jnp.max(scores, axis=-1, keepdims=True)
            ind1 = jnp.argmax(scores, axis=-1)
            factor1 = jnp.maximum(jnp.abs(scores), m1)
            mask1 = jax.lax.stop_gradient((m1 - scores) / factor1 > 2.0 * jitter_eps)
            gates1 = jax.nn.softmax(jnp.where(mask1, NEG_INF, scores), axis=-1)
            mult1 = jnp.take_along_axis(gates1, ind1[:, None], axis=-1)[:, 0]
            E = scores.shape[-1]
            onehot1 = ind1[:, None] == jnp.arange(E)[None, :]
            masked_scores = jnp.where(onehot1, NEG_INF, scores)
            m2 = jnp.max(masked_scores, axis=-1, keepdims=True)
            ind2 = jnp.argmax(masked_scores, axis=-1)
            factor2 = jnp.maximum(jnp.abs(scores), m2)
            mask2 = jax.lax.stop_gradient((m2 - scores) / factor2 > 2.0 * jitter_eps)
            gates2 = jax.nn.softmax(jnp.where(mask2, NEG_INF, masked_scores), axis=-1)
            mult2 = jnp.take_along_axis(gates2, ind2[:, None], axis=-1)[:, 0]
            multiplier = jnp.stack([mult1, mult2], axis=-1)
            selected = jnp.stack([ind1, ind2], axis=-1)
            return (multiplier, selected)
        B, S, H = hidden_states.shape
        E = router_w.shape[0]
        x = hidden_states.reshape(-1, H)
        T = x.shape[0]
        logits = x @ router_w.T
        routing_weights, selected = sparsemixer_eval(logits, JITTER_EPS)
        tok = jnp.arange(T)
        dense_w = jnp.zeros((T, E), dtype=x.dtype)
        dense_w = dense_w.at[tok, selected[:, 0]].add(routing_weights[:, 0])
        dense_w = dense_w.at[tok, selected[:, 1]].add(routing_weights[:, 1])
        out = jnp.zeros_like(x)
        for e in range(E):
            h = jax.nn.silu(x @ w_gate[e].T) * (x @ w_up[e].T)
            out = out + dense_w[:, e:e + 1] * (h @ w_down[e].T)
        return out.reshape(B, S, H)
    x = x + _L0_xattn_ref(_layernorm(x, axis=-1), ctx_1024, ctx_1024, ctx_1024)
    x = x + _L0_attn_ref(_layernorm(x, axis=-1), L0_attn_Wq, L0_attn_Wkv, L0_attn_Wo, L0_attn_norm_w, L0_attn_norm_b, L0_attn_out_norm_w, L0_attn_out_norm_b)
    x = x + _L0_ffn_ref(_layernorm(x, axis=-1), L0_ffn_router_w, L0_ffn_w_gate, L0_ffn_w_up, L0_ffn_w_down)
    return x

_drawn_inputs = setup_inputs


def setup_inputs(seed=0):
    import zlib

    import numpy as np

    out = dict(_drawn_inputs(seed))
    spreads = {'L0_attn_norm_w': (1.0, 0.6),
     'L0_attn_norm_b': (0.0, 0.8),
     'L0_attn_out_norm_w': (1.0, 0.6),
     'L0_attn_out_norm_b': (0.0, 0.8)}
    factors = {'L0_attn_Wq': 8.0,
     'L0_ffn_router_w': 8.0,
     'L0_ffn_w_gate': 8.0,
     'L0_ffn_w_up': 8.0,
     'L0_ffn_w_down': 8.0}
    for name, (base, spread) in spreads.items():
        noise = np.random.default_rng([zlib.crc32(name.encode()), seed]).standard_normal(out[name].shape)
        drawn = base * np.exp(spread * noise) if base else spread * noise
        out[name] = jnp.asarray(drawn.astype(out[name].dtype))
    for name, factor in factors.items():
        out[name] = (out[name] * factor).astype(out[name].dtype)
    return out
```

```python
from contextlib import ExitStack

import concourse.bass as bass
from concourse import mybir

F32 = mybir.dt.float32
F32R = mybir.dt.float32r
ALU = mybir.AluOpType
ACT = mybir.ActivationFunctionType
AX_X = mybir.AxisListType.X

P = 128
EPS = 1e-5
JITTER = 2.0 * 0.01
LOWEST = -3.0e38


def build(nc, x, ctx_in, Wq, Wkv, Wo, norm_w, norm_b, out_norm_w, out_norm_b, routerT, w_gate, w_up, w_down, out):
    B, S, D = x.shape
    L = ctx_in.shape[1]
    E, F, _ = w_gate.shape
    DH = Wkv.shape[1] // 2
    HEADS = Wq.shape[1] // DH
    SCALE = float(DH) ** -0.5
    KD = D // P
    NT = B * S // P
    TB = NT // B
    NC = L // P
    NF = F // P
    T = B * S
    PAIRS = HEADS // 2
    UNITS = HEADS * TB
    assert D == 512 and S == 512 and DH == 64 and KD == TB and NC % 4 == 0 and NF == 8

    x_dram = x.rearrange("b (t p) d -> p (b t) d", p=P)
    out_dram = out.rearrange("b (t p) d -> p (b t) d", p=P)
    ctx_pairs = ctx_in.rearrange("b (j u p) d -> (b j) p u d", u=2, p=P)
    gate_rows = w_gate.rearrange("e (c p) d -> (e c) p d", p=P)
    up_rows = w_up.rearrange("e (c p) d -> (e c) p d", p=P)
    down_half = w_down.rearrange("e (j p) (k f) -> e k p j f", p=P, k=2)

    with ExitStack() as top:
        def sem(name):
            return top.enter_context(nc.semaphore(name))

        def sb(scope, name, shape, dt=F32):
            return scope.enter_context(nc.sbuf_tensor(name, shape, dt))

        def split_sb(scope, name, shape):
            return sb(scope, name + "_hi", shape, F32R), sb(scope, name + "_lo", shape, F32R)

        bank = [top.enter_context(nc.psum_tensor(f"bank{i}", [P, 512], F32)) for i in range(8)]
        T_BANK = bank[0:2]

        x_res = sb(top, "x_res", [P, NT, D])
        xT_hi, xT_lo = split_sb(top, "xT", [P, KD, T])
        ident = sb(top, "ident", [P, P])
        stats = sb(top, "stats", [P, NT, 6])
        mv = sb(top, "mv", [P, NT, 2])
        var_eps = sb(top, "var_eps", [P, NT])
        rstd = sb(top, "rstd", [P, NT])
        neg_half = sb(top, "neg_half", [P, NT])
        rank = sb(top, "rank", [P, E])
        rw_raw = sb(top, "rw_raw", [P, KD, E])

        ab = ExitStack()
        w_raw = sb(ab, "w_raw", [P, KD, D])
        wkv_raw = sb(ab, "wkv_raw", [P, KD, 2 * DH])
        nw_row = sb(ab, "nw_row", [P, D])
        nb_row = sb(ab, "nb_row", [P, D])
        ow_row = sb(ab, "ow_row", [P, D])
        ob_row = sb(ab, "ob_row", [P, D])

        a_ = ExitStack()
        xn_a = sb(a_, "xn_a", [P, NT, D])
        ctx_raw = sb(a_, "ctx_raw", [P, 2, 2, D])
        ctxT_hi, ctxT_lo = split_sb(a_, "ctxT", [P, 2, KD, P])
        ctxN_hi, ctxN_lo = split_sb(a_, "ctxN", [P, 2, D])
        gelu_x = sb(a_, "gelu_x", [P, 2, S])
        hid = sb(a_, "hid", [P, 2, S])
        hidT_hi, hidT_lo = split_sb(a_, "hidT", [P, 2, S])
        a_.close()

        b_ = ExitStack()
        xn_b = sb(b_, "xn_b", [P, NT, D])
        wq_hi, wq_lo = split_sb(b_, "wq", [P, KD, D])
        wo_hi, wo_lo = split_sb(b_, "wo", [P, KD, D])
        wk2_hi, wk2_lo = split_sb(b_, "wk2", [P, KD, 2, DH])
        wv_hi, wv_lo = split_sb(b_, "wv", [P, KD, DH])
        qT_hi, qT_lo = split_sb(b_, "qT", [P, PAIRS, S])
        kT_hi, kT_lo = split_sb(b_, "kT", [P, S])
        vp_hi, vp_lo = split_sb(b_, "vp", [P, TB, 3, DH])
        prob = sb(b_, "prob", [P, 2, S])
        probT_hi, probT_lo = split_sb(b_, "probT", [P, KD, S])
        oT_hi, oT_lo = split_sb(b_, "oT", [P, PAIRS, S])
        neg_max = sb(b_, "neg_max", [P, B * UNITS])
        row_sum = sb(b_, "row_sum", [P, B * UNITS])
        row_inv = sb(b_, "row_inv", [P, B * UNITS])
        y_sb = xn_b
        b_.close()
        ab.close()

        c_ = ExitStack()
        gu_raw = sb(c_, "gu_raw", [P, 2, 2, D])
        down_raw = sb(c_, "down_raw", [P, 2, KD, F // 2])
        rw_hi, rw_lo = split_sb(c_, "rw", [P, KD, E])
        logit = sb(c_, "logit", [P, NT, E])
        r_gap = sb(c_, "r_gap", [P, 2, NT, E])
        r_exp = sb(c_, "r_exp", [P, 2, NT, E])
        r_hot = sb(c_, "r_hot", [P, 2, NT, E])
        r_keep = sb(c_, "r_keep", [P, 2, NT, E])
        r_abs = sb(c_, "r_abs", [P, NT, E])
        r_lim = sb(c_, "r_lim", [P, NT, E])
        r_cand = sb(c_, "r_cand", [P, NT, E])
        r_other = sb(c_, "r_other", [P, NT, E])
        r_rest = sb(c_, "r_rest", [P, NT, E])
        r_red = sb(c_, "r_red", [P, 2, NT])
        r_top = sb(c_, "r_top", [P, 2, NT])
        r_sum = sb(c_, "r_sum", [P, 2, NT])
        r_mult = sb(c_, "r_mult", [P, 2, NT])
        dense_w = sb(c_, "dense_w", [P, NT, E])
        expert_w = sb(c_, "expert_w", [P, NT])
        guT_hi, guT_lo = split_sb(c_, "guT", [P, 2, 2, KD, P])
        dnT_hi, dnT_lo = split_sb(c_, "dnT", [P, NF, D])
        silu_g = sb(c_, "silu_g", [P, 2, S])
        act_h = sb(c_, "act_h", [P, 2, S])
        cn = ExitStack()
        xn_c = sb(cn, "xn_c", [P, NT, D])
        cn.close()
        hT_hi, hT_lo = split_sb(c_, "hT", [P, NF, T])
        c_.close()

        const_ready = sem("const_ready")
        x_loaded = sem("x_loaded")
        wq_loaded, wo_loaded, small_loaded = sem("wq_loaded"), sem("wo_loaded"), sem("small_loaded")
        ln_stat = [sem(f"ln{s}_stat") for s in range(3)]
        ln_var = [sem(f"ln{s}_var") for s in range(3)]
        ln_rstd = [sem(f"ln{s}_rstd") for s in range(3)]
        ln_first = sem("ln1_first")
        ln_scaled = sem("ln1_scaled")
        xn_ready = [sem(f"ln{s}_xn") for s in range(3)]
        xn_turned = [sem(f"ln{s}_turned") for s in range(3)]
        xT_hi_done = [sem(f"ln{s}_hi") for s in range(3)]
        xT_lo_done = [sem(f"ln{s}_lo") for s in range(3)]
        ctx_loaded = [sem("ctx_loaded0"), sem("ctx_loaded1")]
        ctx_turned = sem("ctx_turned")
        ctxT_hi_done, ctxT_lo_done = sem("ctxT_hi_done"), sem("ctxT_lo_done")
        ctxN_hi_done, ctxN_lo_done = sem("ctxN_hi_done"), sem("ctxN_lo_done")
        x1_done, gelu_done, hid_done = sem("x1_done"), sem("gelu_done"), sem("hid_done")
        hidT_hi_done, hidT_lo_done = sem("hidT_hi_done"), sem("hidT_lo_done")
        cross_done = sem("cross_done")
        cross_added = sem("cross_added")
        w_hi_done, w_lo_done, pads_zero = sem("w_hi_done"), sem("w_lo_done"), sem("pads_zero")
        proj_done, proj_hi_done, proj_lo_done = sem("proj_done"), sem("proj_hi_done"), sem("proj_lo_done")
        sim_done, max_done, exp_done = sem("sim_done"), sem("max_done"), sem("exp_done")
        inv_done, prob_done = sem("inv_done"), sem("prob_done")
        prob_turned, probT_hi_done, probT_lo_done = sem("prob_turned"), sem("probT_hi_done"), sem("probT_lo_done")
        pv_done, oT_hi_done, oT_lo_done = sem("pv_done"), sem("oT_hi_done"), sem("oT_lo_done")
        yn_stat, yn_var, yn_rstd, yn_step = sem("yn_stat"), sem("yn_var"), sem("yn_rstd"), sem("yn_step")
        self_added = sem("self_added")
        gu_loaded = [sem("gu_loaded0"), sem("gu_loaded1")]
        down_loaded = [sem("down_loaded0"), sem("down_loaded1")]
        rw_hi_done, rw_lo_done, logits_done = sem("rw_hi_done"), sem("rw_lo_done"), sem("logits_done")
        route_step, route_gap, route_exp = sem("route_step"), sem("route_gap"), sem("route_exp")
        w_turned, wT_hi_done, wT_lo_done = sem("w_turned"), sem("wT_hi_done"), sem("wT_lo_done")
        gate_done, up_done, silu_done, act_done = sem("gate_done"), sem("up_done"), sem("silu_done"), sem("act_done")
        hT_hi_done, hT_lo_done = sem("hT_hi_done"), sem("hT_lo_done")
        down_done, weight_picked, combined = sem("down_done"), sem("weight_picked"), sem("combined")
        stored = sem("stored")

        def f32(ap):
            return ap.bitcast(F32)

        def quarters(b):
            return b[:, :].rearrange("p (c q) -> p c q", c=4)

        GATE, UP, DOWN = range(3)
        GATE_BANK, UP_BANK, Y_BANK = bank[2:4], bank[4:6], bank[6:8]
        X1_BANK, ACC_BANK = bank[2:4], bank[4:8]
        SIM_BANK, O_BANK, M_BANK = bank[2:4], bank[4:6], bank[6:8]
        USES = PAIRS + 1 + TB + TB

        def wT_slot(kind, c):
            if kind == DOWN:
                return tuple(w[:, c, :].rearrange("p (j h) -> p j h", j=KD) for w in (dnT_hi, dnT_lo))
            return guT_hi[:, c % 2, kind], guT_lo[:, c % 2, kind]

        block = top.enter_context(nc.Block())

        @block.sync
        def _(sp):
            for t in range(NT):
                sp.dma_start(x_res[:, t, :], x_dram[:, t, :]).then_inc(x_loaded, 16)

            def load_ctx(j, s):
                sp.dma_start(ctx_raw[:, s], ctx_pairs[bass.ds(j, 1)].rearrange("a p u d -> p (a u) d")).then_inc(ctx_loaded[s], 16)

            for s in range(2):
                load_ctx(s, s)
            sp.dma_start(w_raw[:], Wq.rearrange("(c p) n -> p c n", p=P)).then_inc(wq_loaded, 16)
            sp.dma_start(wkv_raw[:], Wkv.rearrange("(c p) n -> p c n", p=P)).then_inc(small_loaded, 16)
            for row, w in ((nw_row, norm_w), (nb_row, norm_b), (ow_row, out_norm_w), (ob_row, out_norm_b)):
                sp.dma_start(row[:], w.rearrange("(a d) -> a d", a=1).broadcast_to([P, D])).then_inc(small_loaded, 16)
            sp.dma_start(rw_raw[:], routerT.rearrange("(c p) e -> p c e", p=P)).then_inc(small_loaded, 16)
            with sp.Fori(1, B * NC // 4) as i:
                for s in range(2):
                    sp.wait_ge(ctx_turned, 4 * i + 2 * s - 2)
                    sp.wait_ge(ctxN_lo_done, 4 * i + 2 * s - 2)
                    load_ctx(2 * i + s, s)
            sp.wait_ge(w_lo_done, 1)
            sp.dma_start(w_raw[:], Wo.rearrange("(c p) n -> p c n", p=P)).then_inc(wo_loaded, 16)

            sp.wait_ge(self_added, NT)

            def load_experts(e, first):
                for c in range(NF):
                    if c % 4 == 0:
                        k = c // 4
                        if not first:
                            sp.wait_ge(w_turned, 3 * NF * e + 3 * (4 * k - 4))
                        sp.dma_start(down_raw[:, k],
                                     down_half[bass.ds(e, 1), k].rearrange("a p j f -> p (a j) f")).then_inc(down_loaded[k], 16)
                    if not first or c >= 2:
                        sp.wait_ge(w_turned, 3 * NF * e + 3 * (c - 2) + 2)
                    for m, rows in enumerate((gate_rows, up_rows)):
                        sp.dma_start(gu_raw[:, c % 2, m, :],
                                     rows[bass.ds(NF * e + c, 1)].rearrange("a p d -> p (a d)")).then_inc(gu_loaded[c % 2], 16)

            load_experts(0, True)
            with sp.Fori(1, E) as e:
                load_experts(e, False)
            for t in range(NT):
                sp.wait_ge(combined, NT * (E - 1) + t + 1)
                sp.dma_start(out_dram[:, t, :], x_res[:, t, :]).then_inc(stored, 16)
            sp.wait_ge(stored, 16 * NT)

        @block.gpsimd
        def _(pool):
            nc.gpsimd.memset(ident[:], 0.0).then_inc(const_ready, 1)
            nc.gpsimd.memset(neg_half[:], -0.5).then_inc(const_ready, 1)
            for e in range(E):
                nc.gpsimd.memset(rank[:, e:e + 1], float(E - e)).then_inc(const_ready, 1)
            pool.wait_ge(const_ready, 1)
            nc.gpsimd.affine_select(out=ident[:], in_=ident[:], compare_op=ALU.not_equal, fill=1.0,
                                    base=0, pattern=[[-1, P]], channel_multiplier=1).then_inc(const_ready, 1)

            def power(ready, done, n):
                pool.wait_ge(ready, n)
                nc.gpsimd.tensor_tensor(rstd[:], var_eps[:], neg_half[:], ALU.pow).then_inc(done, 1)

            power(ln_var[0], ln_rstd[0], 1)

            def ctx_lo(g, k):
                pool.wait_ge(ctxN_hi_done, g + 1)
                nc.gpsimd.tensor_tensor(ctxN_lo[:, k % 2, :], ctx_raw[:, (k // 2) % 2, k % 2, :],
                                        f32(ctxN_hi[:, k % 2, :]), ALU.subtract).then_inc(ctxN_lo_done, 1)

            with pool.Fori(0, B * NC // 4) as i:
                for k in range(4):
                    ctx_lo(4 * i + k, k)

            pool.wait_ge(cross_done, B * NC)
            nc.gpsimd.memset(f32(vp_hi[:, :, 0, :]), 0.0).then_inc(pads_zero, 1)
            nc.gpsimd.memset(f32(vp_hi[:, :, 2, :]), 0.0).then_inc(pads_zero, 1)
            nc.gpsimd.memset(f32(vp_lo[:, :, 0, :]), 0.0).then_inc(pads_zero, 1)
            nc.gpsimd.memset(f32(vp_lo[:, :, 2, :]), 0.0).then_inc(pads_zero, 1)
            pool.wait_ge(w_hi_done, 1)
            nc.gpsimd.tensor_tensor(wq_lo[:], w_raw[:], f32(wq_hi[:]), ALU.subtract).then_inc(w_lo_done, 1)
            power(ln_var[1], ln_rstd[1], 1)
            pool.wait_ge(w_hi_done, 4)
            nc.gpsimd.tensor_tensor(wv_lo[:], wkv_raw[:, :, DH:], f32(wv_hi[:]), ALU.subtract).then_inc(w_lo_done, 1)
            power(ln_var[1], ln_rstd[1], 2)
            for r in range(2):
                nc.gpsimd.tensor_tensor(wk2_lo[:, :, r, :], wkv_raw[:, :, 0:DH], f32(wk2_hi[:, :, r, :]),
                                        ALU.subtract).then_inc(w_lo_done, 1)
            pool.wait_ge(w_hi_done, 5)
            nc.gpsimd.tensor_tensor(wo_lo[:], w_raw[:], f32(wo_hi[:]), ALU.subtract).then_inc(w_lo_done, 1)
            for b in range(B):
                power(yn_var, yn_rstd, b + 1)
            power(ln_var[2], ln_rstd[2], 1)

        @block.scalar
        def _(act):
            def norm_hi(s):
                for t in range(NT):
                    act.wait_ge(xn_turned[s], t + 1)
                    nc.scalar.activation(xT_hi[:, :, t * P:(t + 1) * P], quarters(T_BANK[t % 2]),
                                         ACT.Copy).then_inc(xT_hi_done[s], 1)

            norm_hi(0)

            def ctxT_hi_step(g, k, first=False):
                act.wait_ge(ctx_turned, g + 1)
                if not first:
                    act.wait_ge(x1_done, g - 1)
                nc.scalar.activation(ctxT_hi[:, k % 2], quarters(T_BANK[k % 2]), ACT.Copy).then_inc(ctxT_hi_done, 1)

            def gelu_step(g, k, first=False):
                act.wait_ge(x1_done, g + 1)
                if not first:
                    act.wait_ge(hid_done, g - 1)
                nc.scalar.activation(gelu_x[:, k % 2, :], X1_BANK[k % 2][:, :], ACT.Gelu_apprx_tanh).then_inc(gelu_done, 1)

            def hid_hi_step(g, k, first=False):
                act.wait_ge(hid_done, g + 1)
                if not first:
                    act.wait_ge(cross_done, g - 1)
                nc.scalar.activation(hidT_hi[:, k % 2, :], hid[:, k % 2, :], ACT.Copy).then_inc(hidT_hi_done, 1)

            for b in range(B):
                g0 = b * NC
                for k in range(2):
                    ctxT_hi_step(g0 + k, k, first=(b == 0))
                gelu_step(g0, 0, first=(b == 0))
                hid_hi_step(g0, 0, first=(b == 0))

                def cross_step(g, k, ahead2=True, ahead1=True, first=False):
                    if ahead2:
                        ctxT_hi_step(g + 2, k + 2)
                    if ahead1:
                        gelu_step(g + 1, k + 1, first)
                        hid_hi_step(g + 1, k + 1, first)

                for k in range(4):
                    cross_step(g0 + k, k, first=(b == 0 and k == 0))
                with act.Fori(1, NC // 4 - 1) as i:
                    for k in range(4):
                        cross_step(4 * i + (g0 + k), k)
                for k in range(4):
                    cross_step(g0 + NC - 4 + k, k, ahead2=k < 2, ahead1=k < 3)

            act.wait_ge(cross_done, B * NC)
            act.wait_ge(wq_loaded, 16)
            nc.scalar.activation(wq_hi[:], w_raw[:], ACT.Copy).then_inc(w_hi_done, 1)
            act.wait_ge(small_loaded, 16 * 6)
            nc.scalar.activation(wv_hi[:], wkv_raw[:, :, DH:], ACT.Copy).then_inc(w_hi_done, 1)
            for r in range(2):
                nc.scalar.activation(wk2_hi[:, :, r, :], wkv_raw[:, :, 0:DH], ACT.Copy).then_inc(w_hi_done, 1)
            act.wait_ge(wo_loaded, 16)
            nc.scalar.activation(wo_hi[:], w_raw[:], ACT.Copy).then_inc(w_hi_done, 1)
            norm_hi(1)

            for b in range(B):
                for m in range(PAIRS):
                    act.wait_ge(proj_done, USES * b + m + 1)
                    nc.scalar.activation(qT_hi[:, m, :], M_BANK[(USES * b + m) % 2][:, :], ACT.Copy,
                                         scale=SCALE).then_inc(proj_hi_done, 1)
                m = PAIRS
                act.wait_ge(proj_done, USES * b + m + 1)
                nc.scalar.activation(kT_hi[:], M_BANK[(USES * b + m) % 2][:, :], ACT.Copy).then_inc(proj_hi_done, 1)
                for t in range(TB):
                    m = PAIRS + 1 + t
                    act.wait_ge(proj_done, USES * b + m + 1)
                    nc.scalar.activation(vp_hi[:, t, 1, :], M_BANK[(USES * b + m) % 2][:, 0:DH],
                                         ACT.Copy).then_inc(proj_hi_done, 1)

                def probT_hi_step(u):
                    v = UNITS * b + u
                    h = HEADS * b + u // TB
                    act.wait_ge(prob_turned, v + 1)
                    if h >= 1:
                        act.wait_ge(pv_done, h)
                    nc.scalar.activation(probT_hi[:, :, (u % TB) * P:(u % TB + 1) * P], quarters(T_BANK[u % 2]),
                                         ACT.Copy).then_inc(probT_hi_done, 1)

                for u in range(UNITS + 5):
                    v = UNITS * b + u
                    if u < UNITS:
                        act.wait_ge(max_done, v + 1)
                        if v >= 2:
                            act.wait_ge(prob_turned, v - 1)
                        nc.scalar.activation(prob[:, u % 2, :], SIM_BANK[u % 2][:, :], ACT.Exp,
                                             bias=neg_max[:, v:v + 1], accum_out=row_sum[:, v:v + 1]).then_inc(exp_done, 1)
                    if 0 <= u - 1 < UNITS:
                        probT_hi_step(u - 1)
                    if u >= 4 and (u - 4) % (2 * TB) == 2 * TB - 1:
                        p = (u - 4) // (2 * TB)
                        act.wait_ge(pv_done, HEADS * b + 2 * p + 2)
                        if b >= 1:
                            act.wait_ge(proj_done, USES * b)
                        nc.scalar.activation(oT_hi[:, p, :], O_BANK[p % 2][:, :], ACT.Copy).then_inc(oT_hi_done, 1)

            act.wait_ge(self_added, NT)
            nc.scalar.activation(rw_hi[:], rw_raw[:], ACT.Copy).then_inc(rw_hi_done, 1)
            norm_hi(2)

            def wT_hi_step(kind, c, q, free_after=None):
                act.wait_ge(w_turned, 3 * q + kind + 1)
                if free_after is not None:
                    act.wait_ge(*free_after)
                n = kind if kind == DOWN else kind
                bank_of = (3 * c + n) % 2
                nc.scalar.activation(wT_slot(kind, c)[0], quarters(T_BANK[bank_of]), ACT.Copy).then_inc(wT_hi_done, 1)

            def silu_step(s, v, first):
                act.wait_ge(gate_done, v + 1)
                if not first:
                    act.wait_ge(act_done, v - 1)
                nc.scalar.activation(silu_g[:, s, :], GATE_BANK[s][:, :], ACT.Silu).then_inc(silu_done, 1)

            def hT_hi_step(c, s, v):
                act.wait_ge(act_done, v + 1)
                nc.scalar.activation(hT_hi[:, c, s * S:(s + 1) * S], act_h[:, s, :], ACT.Copy).then_inc(hT_hi_done, 1)

            def expert(e, first, last):
                for c in range(NF):
                    q = NF * e + c
                    wT_hi_step(DOWN, c, q, None if first else (down_done, NT * e))
                    if not (last and c == NF - 1):
                        free = None if first and c == 0 else (up_done, 2 * q)
                        wT_hi_step(GATE, (c + 1), q + 1, free)
                        wT_hi_step(UP, (c + 1), q + 1)
                    for s in range(2):
                        silu_step(s, 2 * q + s, first and c == 0)
                        hT_hi_step(c, s, 2 * q + s)
                    if first and c == 0:
                        act.wait_ge(route_gap, 1)
                        nc.scalar.activation(r_exp[:], r_gap[:], ACT.Exp, scale=-1.0).then_inc(route_exp, 1)

            wT_hi_step(GATE, 0, 0)
            wT_hi_step(UP, 0, 0)
            expert(0, True, False)
            with act.Fori(1, E - 1) as e:
                expert(e, False, False)
            expert(E - 1, False, True)

        @block.vector
        def _(dve):
            def norm_stats(src, n, stat, base, var_done):
                for t in range(n):
                    nc.vector.bn_stats(stats[:, t, :], src[:, t, :]).then_inc(stat, 1)
                for t in range(n):
                    dve.wait_ge(stat, base + n)
                    nc.vector.bn_aggr(mv[:, t, :], stats[:, t, :]).then_inc(stat, 1)
                dve.wait_ge(stat, base + 2 * n)
                nc.vector.tensor_scalar_add(var_eps[:, 0:n], mv[:, 0:n, 1], EPS).then_inc(var_done, 1)

            def norm_lo(s, t):
                dve.wait_ge(xT_hi_done[s], t + 1)
                nc.vector.tensor_tensor(xT_lo[:, :, t * P:(t + 1) * P], quarters(T_BANK[t % 2]),
                                        f32(xT_hi[:, :, t * P:(t + 1) * P]), ALU.subtract).then_inc(xT_lo_done[s], 1)

            def norm(s, xn):
                norm_stats(x_res, NT, ln_stat[s], 0, ln_var[s])
                dve.wait_ge(ln_rstd[s], 1)
                for t in range(NT):
                    nc.vector.tensor_scalar(xn[:, t, :], x_res[:, t, :], mv[:, t, 0:1], rstd[:, t:t + 1],
                                            ALU.subtract, ALU.mult).then_inc(xn_ready[s], 1)
                    if t >= 1:
                        norm_lo(s, t - 1)
                norm_lo(s, NT - 1)

            dve.wait_ge(x_loaded, 16 * NT)
            dve.wait_ge(const_ready, 3 + E)
            norm(0, xn_a)

            def ctxT_lo_step(g, k):
                dve.wait_ge(ctxT_hi_done, g + 1)
                nc.vector.tensor_tensor(ctxT_lo[:, k % 2], quarters(T_BANK[k % 2]), f32(ctxT_hi[:, k % 2]),
                                        ALU.subtract).then_inc(ctxT_lo_done, 1)

            def ctxN_hi_step(g, k, landed, first=False):
                dve.wait_ge(ctx_loaded[(k // 2) % 2], landed)
                if not first:
                    dve.wait_ge(cross_done, g - 1)
                nc.vector.tensor_copy(ctxN_hi[:, k % 2, :], ctx_raw[:, (k // 2) % 2, k % 2, :]).then_inc(ctxN_hi_done, 1)

            def hid_step(g, k, first=False):
                dve.wait_ge(gelu_done, g + 1)
                if not first:
                    dve.wait_ge(hidT_lo_done, g - 1)
                nc.vector.tensor_tensor(hid[:, k % 2, :], X1_BANK[k % 2][:, :], gelu_x[:, k % 2, :],
                                        ALU.mult).then_inc(hid_done, 1)

            def hid_lo_step(g, k):
                dve.wait_ge(hidT_hi_done, g + 1)
                nc.vector.tensor_tensor(hidT_lo[:, k % 2, :], hid[:, k % 2, :], f32(hidT_hi[:, k % 2, :]),
                                        ALU.subtract).then_inc(hidT_lo_done, 1)

            for b in range(B):
                g0 = b * NC
                l0 = 16 * (g0 // 4)
                for k in range(2):
                    ctxT_lo_step(g0 + k, k)
                ctxN_hi_step(g0, 0, l0 + 16, first=(b == 0))
                hid_step(g0, 0, first=(b == 0))
                hid_lo_step(g0, 0)

                def cross_step(g, k, landed, ahead2=True, ahead1=True, first=False):
                    if ahead2:
                        ctxT_lo_step(g + 2, k + 2)
                    if ahead1:
                        ctxN_hi_step(g + 1, k + 1, landed, first)
                        hid_step(g + 1, k + 1, first)
                        hid_lo_step(g + 1, k + 1)

                for k in range(4):
                    cross_step(g0 + k, k, l0 + 16 * (1 + (k + 1) // 4), first=(b == 0 and k == 0))
                with dve.Fori(1, NC // 4 - 1) as i:
                    for k in range(4):
                        cross_step(4 * i + (g0 + k), k, 16 * i + (l0 + 16 * (1 + (k + 1) // 4)))
                for k in range(4):
                    cross_step(g0 + NC - 4 + k, k, l0 + 4 * NC, ahead2=k < 2, ahead1=k < 3)
                dve.wait_ge(cross_done, NC * (b + 1))
                for t in range(TB):
                    xt = x_res[:, TB * b + t, :]
                    nc.vector.tensor_tensor(xt, ACC_BANK[t][:, :], xt, ALU.add).then_inc(cross_added, 1)

            dve.wait_ge(cross_added, NT)
            norm_stats(x_res, NT, ln_stat[1], 0, ln_var[1])
            dve.wait_ge(ln_rstd[1], 1)
            for t in range(NT):
                nc.vector.tensor_scalar(xn_b[:, t, :], x_res[:, t, :], mv[:, t, 0:1], rstd[:, t:t + 1],
                                        ALU.subtract, ALU.mult).then_inc(ln_first, 1)
            dve.wait_ge(ln_first, NT)
            norm_stats(xn_b, NT, ln_stat[1], 2 * NT, ln_var[1])
            dve.wait_ge(small_loaded, 16 * 6)
            for t in range(NT):
                nc.vector.scalar_tensor_tensor(xn_b[:, t, :], xn_b[:, t, :], mv[:, t, 0:1], nw_row[:],
                                               ALU.subtract, ALU.mult).then_inc(ln_scaled, 1)
            dve.wait_ge(ln_rstd[1], 2)
            for t in range(NT):
                dve.wait_ge(ln_scaled, t + 1)
                nc.vector.scalar_tensor_tensor(xn_b[:, t, :], xn_b[:, t, :], rstd[:, t:t + 1], nb_row[:],
                                               ALU.mult, ALU.add).then_inc(xn_ready[1], 1)
                if t >= 1:
                    norm_lo(1, t - 1)
            norm_lo(1, NT - 1)

            for b in range(B):
                done = (PAIRS + 1 + TB) * b
                for m in range(PAIRS):
                    dve.wait_ge(proj_hi_done, done + m + 1)
                    nc.vector.scalar_tensor_tensor(qT_lo[:, m, :], M_BANK[(USES * b + m) % 2][:, :], SCALE,
                                                   f32(qT_hi[:, m, :]), ALU.mult, ALU.subtract).then_inc(proj_lo_done, 1)
                m = PAIRS
                dve.wait_ge(proj_hi_done, done + m + 1)
                nc.vector.tensor_tensor(kT_lo[:], M_BANK[(USES * b + m) % 2][:, :], f32(kT_hi[:]),
                                        ALU.subtract).then_inc(proj_lo_done, 1)
                for t in range(TB):
                    m = PAIRS + 1 + t
                    dve.wait_ge(proj_hi_done, done + m + 1)
                    nc.vector.tensor_tensor(vp_lo[:, t, 1, :], M_BANK[(USES * b + m) % 2][:, 0:DH],
                                            f32(vp_hi[:, t, 1, :]), ALU.subtract).then_inc(proj_lo_done, 1)

                for u in range(UNITS + 5):
                    v = UNITS * b + u
                    if u < UNITS:
                        dve.wait_ge(sim_done, v + 1)
                        nc.vector.tensor_reduce(neg_max[:, v:v + 1], SIM_BANK[u % 2][:, :], AX_X, ALU.max,
                                                negate=True).then_inc(max_done, 1)
                    if 0 <= u - 1 < UNITS:
                        w = v - 1
                        dve.wait_ge(exp_done, w + 1)
                        nc.vector.reciprocal(row_inv[:, w:w + 1], row_sum[:, w:w + 1]).then_inc(inv_done, 1)
                        dve.wait_ge(inv_done, w + 1)
                        nc.vector.tensor_scalar(prob[:, (u - 1) % 2, :], prob[:, (u - 1) % 2, :], row_inv[:, w:w + 1],
                                                None, ALU.mult).then_inc(prob_done, 1)
                    if 0 <= u - 2 < UNITS:
                        w, i = v - 2, (u - 2) % TB
                        dve.wait_ge(probT_hi_done, w + 1)
                        nc.vector.tensor_tensor(probT_lo[:, :, i * P:(i + 1) * P], quarters(T_BANK[u % 2]),
                                                f32(probT_hi[:, :, i * P:(i + 1) * P]),
                                                ALU.subtract).then_inc(probT_lo_done, 1)
                    if u >= 4 and (u - 4) % (2 * TB) == 2 * TB - 1:
                        p = (u - 4) // (2 * TB)
                        dve.wait_ge(oT_hi_done, PAIRS * b + p + 1)
                        nc.vector.tensor_tensor(oT_lo[:, p, :], O_BANK[p % 2][:, :], f32(oT_hi[:, p, :]),
                                                ALU.subtract).then_inc(oT_lo_done, 1)

                for t in range(TB):
                    m = PAIRS + 1 + TB + t
                    dve.wait_ge(proj_done, USES * b + m + 1)
                    nc.vector.tensor_copy(y_sb[:, t, :], M_BANK[(USES * b + m) % 2][:, :]).then_inc(proj_lo_done, 1)
                dve.wait_ge(proj_lo_done, USES * (b + 1))
                norm_stats(y_sb, TB, yn_stat, 2 * TB * b, yn_var)
                step = 2 * TB * b
                for t in range(TB):
                    nc.vector.scalar_tensor_tensor(y_sb[:, t, :], y_sb[:, t, :], mv[:, t, 0:1], ow_row[:],
                                                   ALU.subtract, ALU.mult).then_inc(yn_step, 1)
                dve.wait_ge(yn_rstd, b + 1)
                for t in range(TB):
                    dve.wait_ge(yn_step, step + t + 1)
                    nc.vector.scalar_tensor_tensor(y_sb[:, t, :], y_sb[:, t, :], rstd[:, t:t + 1], ob_row[:],
                                                   ALU.mult, ALU.add).then_inc(yn_step, 1)
                for t in range(TB):
                    xt = x_res[:, TB * b + t, :]
                    dve.wait_ge(yn_step, step + TB + t + 1)
                    nc.vector.tensor_tensor(xt, xt, y_sb[:, t, :], ALU.add).then_inc(self_added, 1)

            dve.wait_ge(self_added, NT)
            norm(2, xn_c)
            dve.wait_ge(rw_hi_done, 1)
            nc.vector.tensor_tensor(rw_lo[:], rw_raw[:], f32(rw_hi[:]), ALU.subtract).then_inc(rw_lo_done, 1)

            def over_experts(ap):
                return ap.unsqueeze(2).broadcast_to([P, NT, E])

            def route():
                step = [0]

                def then(ins):
                    step[0] += 1
                    ins.then_inc(route_step, 1)
                    dve.wait_ge(route_step, step[0])

                V = nc.vector
                first, second = 0, 1
                ranks = rank[:].unsqueeze(1).broadcast_to([P, NT, E])
                dve.wait_ge(logits_done, NT)
                then(V.tensor_copy(logit[:], Y_BANK[0][:, 0:NT * E].rearrange("p (t e) -> p t e", e=E)))
                then(V.scalar_tensor_tensor(r_abs[:], logit[:], -1.0, logit[:], ALU.mult, ALU.max))
                for n, score in ((first, logit), (second, r_rest)):
                    top_b = over_experts(r_top[:, n, :])
                    then(V.tensor_reduce(r_top[:, n, :], score[:], AX_X, ALU.max))
                    then(V.tensor_tensor(r_cand[:], score[:], top_b, ALU.is_ge))
                    then(V.tensor_tensor(r_cand[:], r_cand[:], ranks, ALU.mult))
                    then(V.tensor_reduce(r_red[:, n, :], r_cand[:], AX_X, ALU.max))
                    then(V.tensor_tensor(r_hot[:, n], r_cand[:], over_experts(r_red[:, n, :]), ALU.is_equal))
                    then(V.tensor_tensor(r_gap[:, n], top_b, logit[:], ALU.subtract))
                    then(V.tensor_tensor(r_lim[:], r_abs[:], top_b, ALU.max))
                    then(V.scalar_tensor_tensor(r_keep[:, n], r_lim[:], JITTER, r_gap[:, n], ALU.mult, ALU.is_ge))
                    if n == first:
                        then(V.tensor_scalar(r_other[:], r_hot[:, n], -1.0, 1.0, ALU.mult, ALU.add))
                        then(V.tensor_tensor(r_rest[:], logit[:], r_other[:], ALU.mult))
                        then(V.scalar_tensor_tensor(r_rest[:], r_hot[:, n], LOWEST, r_rest[:], ALU.mult, ALU.add))
                then(V.tensor_tensor(r_keep[:, second], r_keep[:, second], r_other[:], ALU.mult))
                V.tensor_scalar_max(r_gap[:, second], r_gap[:, second], 0.0).then_inc(route_gap, 1)
                dve.wait_ge(route_exp, 1)
                then(V.tensor_tensor(r_keep[:], r_keep[:], r_exp[:], ALU.mult))
                then(V.tensor_reduce(r_sum[:], r_keep[:], AX_X, ALU.add))
                then(V.reciprocal(r_mult[:], r_sum[:]))
                for n in (first, second):
                    then(V.tensor_tensor(r_hot[:, n], r_hot[:, n], over_experts(r_mult[:, n, :]), ALU.mult))
                then(V.tensor_tensor(dense_w[:], r_hot[:, first], r_hot[:, second], ALU.add))

            def wT_lo_step(kind, c, q):
                dve.wait_ge(wT_hi_done, 3 * q + kind + 1)
                hi, lo = wT_slot(kind, c)
                nc.vector.tensor_tensor(lo, quarters(T_BANK[(3 * c + kind) % 2]), f32(hi),
                                        ALU.subtract).then_inc(wT_lo_done, 1)

            def hidden_step(c, s, v, first):
                dve.wait_ge(silu_done, v + 1)
                dve.wait_ge(up_done, v + 1)
                if not first:
                    dve.wait_ge(hT_lo_done, v - 1)
                nc.vector.tensor_tensor(act_h[:, s, :], UP_BANK[s][:, :], silu_g[:, s, :], ALU.mult).then_inc(act_done, 1)
                dve.wait_ge(hT_hi_done, v + 1)
                nc.vector.tensor_tensor(hT_lo[:, c, s * S:(s + 1) * S], act_h[:, s, :],
                                        f32(hT_hi[:, c, s * S:(s + 1) * S]), ALU.subtract).then_inc(hT_lo_done, 1)

            def expert(e, first, last):
                for c in range(NF):
                    q = NF * e + c
                    wT_lo_step(DOWN, c, q)
                    if not (last and c == NF - 1):
                        wT_lo_step(GATE, c + 1, q + 1)
                        wT_lo_step(UP, c + 1, q + 1)
                    for s in range(2):
                        hidden_step(c, s, 2 * q + s, first and c == 0)
                    if first and c == 0:
                        route()
                if not first:
                    dve.wait_ge(combined, NT * e)
                nc.vector.tensor_copy(expert_w[:].unsqueeze(2), dense_w[:, :, bass.ds(e, 1)]).then_inc(weight_picked, 1)
                dve.wait_ge(weight_picked, e + 1)
                for t in range(NT):
                    dve.wait_ge(down_done, NT * e + (t + 1))
                    xt = x_res[:, t, :]
                    nc.vector.scalar_tensor_tensor(xt, Y_BANK[t % 2][:, :], expert_w[:, t:t + 1], xt,
                                                   ALU.mult, ALU.add).then_inc(combined, 1)

            wT_lo_step(GATE, 0, 0)
            wT_lo_step(UP, 0, 0)
            expert(0, True, False)
            with dve.Fori(1, E - 1) as e:
                expert(e, False, False)
            expert(E - 1, False, True)

        @block.tensor
        def _(pe):
            def product(out_ap, pairs, start=True, stop=True):
                n = len(pairs)
                for i, ((l_hi, l_lo), (r_hi, r_lo)) in enumerate(pairs):
                    nc.tensor.matmul(out_ap, l_lo, r_hi, start=start and i == 0, stop=False)
                    nc.tensor.matmul(out_ap, l_hi, r_lo, start=False, stop=False)
                    last = nc.tensor.matmul(out_ap, l_hi, r_hi, start=False, stop=stop and i == n - 1)
                return last

            def turn(dst, blocks):
                for i, blk in enumerate(blocks):
                    last = nc.tensor.transpose(dst[:, i * P:(i + 1) * P], blk, ident[:])
                return last

            def norm_turn(s, xn):
                for t in range(NT):
                    pe.wait_ge(xn_ready[s], t + 1)
                    if t >= 2:
                        pe.wait_ge(xT_lo_done[s], t - 1)
                    turn(T_BANK[t % 2], [xn[:, t, c * P:(c + 1) * P] for c in range(KD)]).then_inc(xn_turned[s], 1)
                pe.wait_ge(xT_lo_done[s], NT)

            def xT_cols(c, lo, n):
                return xT_hi[:, c, lo:lo + n], xT_lo[:, c, lo:lo + n]

            pe.wait_ge(const_ready, 3 + E)
            norm_turn(0, xn_a)

            def ctx_turn(g, k, landed, first=False):
                pe.wait_ge(ctx_loaded[(k // 2) % 2], landed)
                if not first:
                    pe.wait_ge(ctxT_lo_done, g - 1)
                turn(T_BANK[k % 2], [ctx_raw[:, (k // 2) % 2, k % 2, c * P:(c + 1) * P]
                                     for c in range(KD)]).then_inc(ctx_turned, 1)

            def x1_step(b, g, k, first=False):
                pe.wait_ge(ctxT_lo_done, g + 1)
                if not first:
                    pe.wait_ge(hid_done, g - 1)
                product(X1_BANK[k % 2][:, :],
                        [((ctxT_hi[:, k % 2, c, :], ctxT_lo[:, k % 2, c, :]), xT_cols(c, b * S, S))
                         for c in range(KD)]).then_inc(x1_done, 1)

            def cross_out(g, k, start, stop):
                pe.wait_ge(hidT_lo_done, g + 1)
                pe.wait_ge(ctxN_lo_done, g + 1)
                for t in range(TB):
                    cols = slice(t * P, (t + 1) * P)
                    last = product(ACC_BANK[t][:, :],
                                   [((hidT_hi[:, k % 2, cols], hidT_lo[:, k % 2, cols]),
                                     (ctxN_hi[:, k % 2, :], ctxN_lo[:, k % 2, :]))], start=start, stop=stop)
                last.then_inc(cross_done, 1)

            for b in range(B):
                g0 = b * NC
                l0 = 16 * (g0 // 4)
                for k in range(2):
                    ctx_turn(g0 + k, k, l0 + 16, first=(b == 0))
                x1_step(b, g0, 0, first=(b == 0))
                if b >= 1:
                    pe.wait_ge(cross_added, TB * b)

                def cross_step(g, k, landed, ahead2=True, ahead1=True, start=False, stop=False, first=False):
                    if ahead2:
                        ctx_turn(g + 2, k + 2, landed)
                    if ahead1:
                        x1_step(b, g + 1, k + 1, first)
                    cross_out(g, k, start, stop)

                for k in range(4):
                    cross_step(g0 + k, k, l0 + 16 * (1 + (k + 2) // 4), start=(k == 0), first=(b == 0 and k == 0))
                with pe.Fori(1, NC // 4 - 1) as i:
                    for k in range(4):
                        cross_step(4 * i + (g0 + k), k, 16 * i + (l0 + 16 * (1 + (k + 2) // 4)))
                for k in range(4):
                    cross_step(g0 + NC - 4 + k, k, l0 + 4 * NC, ahead2=k < 2, ahead1=k < 3, stop=(k == 3))

            norm_turn(1, xn_b)
            pe.wait_ge(pads_zero, 4)
            pe.wait_ge(w_lo_done, 5)
            for b in range(B):
                def use_bank(m):
                    n = USES * b + m
                    if n >= 2:
                        pe.wait_ge(proj_lo_done, n - 1)
                    return M_BANK[n % 2]

                for p in range(PAIRS):
                    product(use_bank(p)[:, :],
                            [((wq_hi[:, c, p * P:(p + 1) * P], wq_lo[:, c, p * P:(p + 1) * P]), xT_cols(c, b * S, S))
                             for c in range(KD)]).then_inc(proj_done, 1)
                product(use_bank(PAIRS)[:, :],
                        [((wk2_hi[:, c].rearrange("p r d -> p (r d)"), wk2_lo[:, c].rearrange("p r d -> p (r d)")),
                          xT_cols(c, b * S, S)) for c in range(KD)]).then_inc(proj_done, 1)
                for t in range(TB):
                    product(use_bank(PAIRS + 1 + t)[:, 0:DH],
                            [(xT_cols(c, b * S + t * P, P), (wv_hi[:, c, :], wv_lo[:, c, :]))
                             for c in range(KD)]).then_inc(proj_done, 1)
                pe.wait_ge(proj_lo_done, USES * b + PAIRS + 1 + TB)

                for u in range(UNITS + 4):
                    v = UNITS * b + u
                    if u < UNITS:
                        h, i = u // TB, u % TB
                        half = slice((h % 2) * DH, (h % 2) * DH + DH)
                        if v >= 2:
                            pe.wait_ge(exp_done, v - 1)
                        cols = slice(i * P, (i + 1) * P)
                        product(SIM_BANK[u % 2][:, :],
                                [((qT_hi[half, h // 2, cols], qT_lo[half, h // 2, cols]),
                                  (kT_hi[half, :], kT_lo[half, :]))]).then_inc(sim_done, 1)
                    if 0 <= u - 1 < UNITS:
                        w = v - 1
                        pe.wait_ge(prob_done, w + 1)
                        if w >= 2:
                            pe.wait_ge(probT_lo_done, w - 1)
                        turn(T_BANK[(u - 1) % 2],
                             [prob[:, (u - 1) % 2, j * P:(j + 1) * P] for j in range(KD)]).then_inc(prob_turned, 1)
                    if u >= 3 and (u - 3) % TB == TB - 1:
                        h = (u - 3) // TB
                        pe.wait_ge(probT_lo_done, TB * (HEADS * b + h + 1))
                        n = PAIRS * b + h // 2
                        if h % 2 == 0 and n >= 2:
                            pe.wait_ge(oT_lo_done, n - 1)
                        pad = slice(1, 3) if h % 2 == 0 else slice(0, 2)
                        product(O_BANK[(h // 2) % 2][:, :],
                                [((vp_hi[:, j, pad].rearrange("p a d -> p (a d)"), vp_lo[:, j, pad].rearrange("p a d -> p (a d)")),
                                  (probT_hi[:, j, :], probT_lo[:, j, :])) for j in range(KD)],
                                start=h % 2 == 0, stop=h % 2 == 1).then_inc(pv_done, 1)
                pe.wait_ge(oT_lo_done, PAIRS * (b + 1))
                for t in range(TB):
                    product(use_bank(PAIRS + 1 + TB + t)[:, :],
                            [((oT_hi[:, p, t * P:(t + 1) * P], oT_lo[:, p, t * P:(t + 1) * P]),
                              (wo_hi[:, p, :], wo_lo[:, p, :])) for p in range(PAIRS)]).then_inc(proj_done, 1)

            norm_turn(2, xn_c)
            pe.wait_ge(rw_lo_done, 1)
            for t in range(NT):
                product(Y_BANK[0][:, t * E:(t + 1) * E],
                        [(xT_cols(c, t * P, P), (rw_hi[:, c, :], rw_lo[:, c, :])) for c in range(KD)]).then_inc(logits_done, 1)

            def w_turn(kind, c, q, landed=None, first=False):
                if kind == DOWN:
                    src = [down_raw[:, (c // 4) % 2, j, (c % 4) * P:(c % 4 + 1) * P] for j in range(KD)]
                else:
                    src = [gu_raw[:, c % 2, kind, j * P:(j + 1) * P] for j in range(KD)]
                if landed is not None:
                    pe.wait_ge(*landed)
                if not first:
                    pe.wait_ge(wT_lo_done, 3 * q + kind - 1)
                turn(T_BANK[(3 * c + kind) % 2], src).then_inc(w_turned, 1)

            def hidden(kind, c, s, q, first):
                banks, done = ((GATE_BANK, gate_done), (UP_BANK, up_done))[kind]
                if kind == GATE and not first:
                    pe.wait_ge(act_done, 2 * q + s - 1)
                product(banks[s][:, :],
                        [((guT_hi[:, c % 2, kind, j, :], guT_lo[:, c % 2, kind, j, :]), xT_cols(j, s * S, S))
                         for j in range(KD)]).then_inc(done, 1)

            def expert(e, first, last):
                for c in range(NF):
                    q = NF * e + c
                    ahead = not (last and c == NF - 1)
                    landed = 32 * (4 * e + (c + 1) // 2 + 1)
                    w_turn(DOWN, c, q, (down_loaded[c // 4], 16 * (e + 1)) if c % 4 == 0 else None)
                    if ahead:
                        w_turn(GATE, c + 1, q + 1, (gu_loaded[(c + 1) % 2], landed))
                    pe.wait_ge(wT_lo_done, 3 * q + 2)
                    hidden(GATE, c, 0, q, first and c == 0)
                    if ahead:
                        w_turn(UP, c + 1, q + 1)
                    hidden(UP, c, 0, q, first and c == 0)
                    hidden(GATE, c, 1, q, first and c == 0)
                    hidden(UP, c, 1, q, first and c == 0)
                for t in range(NT):
                    if t == 0:
                        pe.wait_ge(wT_lo_done, 3 * (NF * e + NF))
                        pe.wait_ge(hT_lo_done, 2 * (NF * e + NF) - 1)
                    if t == NT // 2:
                        pe.wait_ge(hT_lo_done, 2 * (NF * e + NF))
                    if not (first and t < 2):
                        pe.wait_ge(combined, NT * e + (t - 1))
                    cols = slice(t * P, (t + 1) * P)
                    product(Y_BANK[t % 2][:, :],
                            [((hT_hi[:, c, cols], hT_lo[:, c, cols]), (dnT_hi[:, c, :], dnT_lo[:, c, :]))
                             for c in range(NF)]).then_inc(down_done, 1)

            w_turn(GATE, 0, 0, (gu_loaded[0], 32), first=True)
            w_turn(UP, 0, 0, first=True)
            expert(0, True, False)
            with pe.Fori(1, E - 1) as e:
                expert(e, False, False)
            expert(E - 1, False, True)


_INS = ["x", "ctx_1024", "L0_attn_Wq", "L0_attn_Wkv", "L0_attn_Wo", "L0_attn_norm_w", "L0_attn_norm_b",
        "L0_attn_out_norm_w", "L0_attn_out_norm_b", "L0_ffn_router_w", "L0_ffn_w_gate", "L0_ffn_w_up", "L0_ffn_w_down"]


def kernel(**inputs):
    import numpy as _np
    import concourse.bacc as _bacc
    from concourse import mybir as _mybir
    from concourse.bass_utils import run_bass_kernel_spmd as _run

    nc = _bacc.Bacc("TRN2", target_bir_lowering=False, num_devices=1)
    arrays, args = {}, []
    for name in _INS:
        a = inputs[name].T if name == "L0_ffn_router_w" else inputs[name]
        a = _np.ascontiguousarray(a)
        arrays[f"in_{name}"] = a
        args.append(nc.dram_tensor(f"in_{name}", a.shape, _mybir.dt.from_np(a.dtype), kind="ExternalInput").ap())
    out = nc.dram_tensor("out_x", inputs["x"].shape, F32, kind="ExternalOutput").ap()
    build(nc, *args, out)
    r = _run(nc, [arrays], core_ids=[0])
    return r.results[0]["out_x"]
```

```python
from contextlib import ExitStack

import concourse.bass as bass
from concourse import mybir

F32 = mybir.dt.float32
F32R = mybir.dt.float32r
ALU = mybir.AluOpType
ACT = mybir.ActivationFunctionType
AX_X = mybir.AxisListType.X

P = 128
EPS = 1e-5
JITTER = 2.0 * 0.01
LOWEST = -3.0e38


def build(nc, x, ctxN_in, ctxT_in, Wq, Wkv, Wo, norm_w, norm_b, out_norm_w, out_norm_b, routerT, gate_upT, downT, out):
    B, S, D = x.shape
    L = ctxN_in.shape[1]
    E, NF = gate_upT.shape[:2]
    DH = Wkv.shape[1] // 2
    HEADS = Wq.shape[1] // DH
    SCALE = float(DH) ** -0.5
    KD = D // P
    NT = B * S // P
    TB = NT // B
    NC = L // P
    T = B * S
    PAIRS = HEADS // 2
    UNITS = HEADS * TB
    assert B == 2 and D == 512 and S == 512 and DH == 64 and KD == TB and NC % 4 == 0 and NF == 8
    HEAD_STEPS = (4, 8)

    x_dram = x.rearrange("b (t p) d -> p (b t) d", p=P)
    out_dram = out.rearrange("b (t p) d -> p (b t) d", p=P)
    ctxN_pairs = ctxN_in.rearrange("b (j u p) d -> (b j) p u d", u=2, p=P)

    with ExitStack() as top:
        def sem(name):
            return top.enter_context(nc.semaphore(name))

        def sb(scope, name, shape, dt=F32):
            return scope.enter_context(nc.sbuf_tensor(name, shape, dt))

        def split_sb(scope, name, shape):
            return sb(scope, name + "_hi", shape, F32R), sb(scope, name + "_lo", shape, F32R)

        bank = [top.enter_context(nc.psum_tensor(f"bank{i}", [P, 512], F32)) for i in range(8)]
        TURN = bank[0:2]
        X1, ACC = bank[2:4], bank[4:8]
        SIM, HEAD_OUT, PROJ = bank[2:4], bank[4:6], bank[6:8]
        Y_OF = (bank[0:4], bank[0:2] + bank[6:8])
        GATE, UP, DOWN_OUT = bank[2:4], bank[4:6], bank[6:8]

        x_res = sb(top, "x_res", [P, NT, D])
        xT_hi, xT_lo = split_sb(top, "xT", [P, KD, T])
        xn = sb(top, "xn", [P, TB, D])
        ident = sb(top, "ident", [P, P])
        rank = sb(top, "rank", [P, E])
        neg_half = sb(top, "neg_half", [P, TB])
        rw_raw = sb(top, "rw_raw", [P, KD, E])
        rw_hi, rw_lo = split_sb(top, "rw", [P, KD, E])
        NORMS = ("a", "b", "b2", "c", "y")
        stats = {n: sb(top, f"stats_{n}", [P, NT, 6]) for n in NORMS}
        mv = {n: sb(top, f"mv_{n}", [P, NT, 2]) for n in NORMS}
        var_eps = {n: sb(top, f"var_eps_{n}", [P, NT]) for n in NORMS}
        rstd = {n: sb(top, f"rstd_{n}", [P, NT]) for n in NORMS}
        logit = sb(top, "logit", [P, NT, E])
        r_gap = sb(top, "r_gap", [P, 2, NT, E])
        r_exp = sb(top, "r_exp", [P, 2, NT, E])
        r_hot = sb(top, "r_hot", [P, 2, NT, E])
        r_keep = sb(top, "r_keep", [P, 2, NT, E])
        r_tmp = [sb(top, f"r_tmp{i}", [P, NT, E]) for i in range(5)]
        r_top = sb(top, "r_top", [P, 2, NT])
        r_red = sb(top, "r_red", [P, 2, NT])
        r_sum = sb(top, "r_sum", [P, 2, NT])
        r_mult = sb(top, "r_mult", [P, 2, NT])
        dense_w = sb(top, "dense_w", [P, NT, E])
        expert_w = sb(top, "expert_w", [P, NT])
        activated = sb(top, "activated", [P, 2, S])
        hid = sb(top, "hid", [P, 2, S])
        wo_raw = sb(top, "wo_raw", [P, KD, D])
        y_sb = wo_raw
        down_raw = wo_raw

        w1 = ExitStack()
        wq_hi, wq_lo = split_sb(w1, "wq", [P, KD, D])
        wk2_hi, wk2_lo = split_sb(w1, "wk2", [P, KD, 2, DH])
        wv_hi, wv_lo = split_sb(w1, "wv", [P, KD, DH])
        w1.close()
        gu_raw = sb(top, "gu_raw", [P, 2, 2, KD, P])
        guT_hi, guT_lo = split_sb(top, "guT", [P, 2, 2, KD, P])

        ab = ExitStack()
        w_raw = sb(ab, "w_raw", [P, KD, D])
        wkv_raw = sb(ab, "wkv_raw", [P, KD, 2 * DH])
        nw_row = sb(ab, "nw_row", [P, D])
        nb_row = sb(ab, "nb_row", [P, D])
        ow_row = sb(ab, "ow_row", [P, D])
        ob_row = sb(ab, "ob_row", [P, D])
        wo_hi, wo_lo = split_sb(ab, "wo", [P, KD, D])
        a_ = ExitStack()
        ctxT_raw = sb(a_, "ctxT_raw", [P, 2, KD, 2 * P])
        ctxN_raw = sb(a_, "ctxN_raw", [P, 2, 2, D])
        ctxT_hi, ctxT_lo = split_sb(a_, "ctxT", [P, 2, KD, P])
        ctxN_hi, ctxN_lo = split_sb(a_, "ctxN", [P, 2, D])
        hidT_hi, hidT_lo = split_sb(a_, "hidT", [P, 2, S])
        a_.close()
        b_ = ExitStack()
        q_o = sb(b_, "q_o", [P, PAIRS, 2, S], F32R)
        kT_hi, kT_lo = split_sb(b_, "kT", [P, S])
        vp_hi, vp_lo = split_sb(b_, "vp", [P, TB, 3, DH])
        prob = sb(b_, "prob", [P, 4, S])
        probT_hi, probT_lo = split_sb(b_, "probT", [P, 2, KD, S])
        neg_max = sb(b_, "neg_max", [P, B * UNITS])
        row_sum = sb(b_, "row_sum", [P, B * UNITS])
        row_inv = sb(b_, "row_inv", [P, B * UNITS])
        b_.close()
        ab.close()
        c_ = ExitStack()
        dnT_hi, dnT_lo = split_sb(c_, "dnT", [P, NF, D])
        hT_hi, hT_lo = split_sb(c_, "hT", [P, NF, T])
        c_.close()

        const_ready = sem("const_ready")
        x_loaded = [sem("x_loaded0"), sem("x_loaded1")]
        w_loaded, small_loaded = sem("w_loaded"), sem("small_loaded")
        norm_stat = {n: sem(f"norm_{n}_stat") for n in NORMS}
        norm_var = {n: sem(f"norm_{n}_var") for n in NORMS}
        norm_rstd = {n: sem(f"norm_{n}_rstd") for n in NORMS}
        b_plain, b_scaled = sem("norm_b_plain"), sem("norm_b_scaled")
        y_scaled, y_normed = sem("norm_y_scaled"), sem("norm_y_done")
        xn_ready = {n: sem(f"xn_{n}_ready") for n in "abc"}
        xn_turned = {n: sem(f"xn_{n}_turned") for n in "abc"}
        xT_hi_done = {n: sem(f"xT_{n}_hi") for n in "abc"}
        xT_lo_done = {n: sem(f"xT_{n}_lo") for n in "abc"}
        ctxT_loaded = [sem("ctxT_loaded0"), sem("ctxT_loaded1")]
        ctxN_loaded = [sem("ctxN_loaded0"), sem("ctxN_loaded1")]
        ctxT_hi_done, ctxT_lo_done = sem("ctxT_hi_done"), sem("ctxT_lo_done")
        ctxN_hi_done, ctxN_lo_done = sem("ctxN_hi_done"), sem("ctxN_lo_done")
        x1_done, gelu_done, hid_done = sem("x1_done"), sem("gelu_done"), sem("hid_done")
        hidT_hi_done, hidT_lo_done = sem("hidT_hi_done"), sem("hidT_lo_done")
        cross_done, cross_added = sem("cross_done"), sem("cross_added")
        w_hi_done, w_lo_done, pads_zero = sem("w_hi_done"), sem("w_lo_done"), sem("pads_zero")
        proj_done, proj_hi_done, proj_lo_done = sem("proj_done"), sem("proj_hi_done"), sem("proj_lo_done")
        sim_done, max_done, exp_done = sem("sim_done"), sem("max_done"), sem("exp_done")
        inv_done, prob_done = sem("inv_done"), sem("prob_done")
        prob_turned, probT_hi_done, probT_lo_done = sem("prob_turned"), sem("probT_hi_done"), sem("probT_lo_done")
        pv_done, oT_hi_done, oT_lo_done = sem("pv_done"), sem("oT_hi_done"), sem("oT_lo_done")
        y_done, self_added = sem("y_done"), sem("self_added")
        gu_loaded = [sem("gu_loaded0"), sem("gu_loaded1")]
        down_loaded = [sem("down_loaded0"), sem("down_loaded1")]
        rw_hi_done, rw_lo_done, logits_done = sem("rw_hi_done"), sem("rw_lo_done"), sem("logits_done")
        route_step, route_gap, route_exp = sem("route_step"), sem("route_gap"), sem("route_exp")
        guT_hi_done, guT_lo_done = sem("guT_hi_done"), sem("guT_lo_done")
        dnT_hi_done, dnT_lo_done = sem("dnT_hi_done"), sem("dnT_lo_done")
        gate_done, up_done, silu_done, act_done = sem("gate_done"), sem("up_done"), sem("silu_done"), sem("act_done")
        hT_hi_done, hT_lo_done = sem("hT_hi_done"), sem("hT_lo_done")
        down_done, weight_picked, combined = sem("down_done"), sem("weight_picked"), sem("combined")
        stored = sem("stored")

        def f32(ap):
            return ap.bitcast(F32)

        def quarters(b):
            return b[:, :].rearrange("p (c q) -> p c q", c=4)

        def tile_cols(t):
            return slice(t * P, (t + 1) * P)

        USES = 1 + TB + PAIRS

        TURN_LAG, LO_LAG, PV_LAG = 3, 4, 5
        PIPE = UNITS + PV_LAG + 4

        def pair_out(u):
            w = u - PV_LAG - 4
            return w // (2 * TB) if w >= 0 and w % (2 * TB) == 2 * TB - 1 else None

        def behind(u, first):
            t = (u - first) // 2
            return t if u >= first and (u - first) % 2 == 0 and t < TB else None
        BEHIND = (1, 7)

        def hidden_order(e_first):
            order = [(c, s) for c in range(NF) for s in range(2)]
            if e_first:
                order[1], order[2] = order[2], order[1]
            return order

        block = top.enter_context(nc.Block())

        @block.sync
        def _(sp):
            def load_ctx(j, s):
                sp.dma_start(ctxT_raw[:, s], ctxT_in[bass.ds(j, 1)].rearrange("a p c f -> p (a c) f")).then_inc(ctxT_loaded[s], 16)
                sp.dma_start(ctxN_raw[:, s], ctxN_pairs[bass.ds(j, 1)].rearrange("a p u d -> p (a u) d")).then_inc(ctxN_loaded[s], 16)

            sp.dma_start(x_res[:, 0:TB, :], x_dram[:, 0:TB, :]).then_inc(x_loaded[0], 16)
            load_ctx(0, 0)
            sp.dma_start(x_res[:, TB:NT, :], x_dram[:, TB:NT, :]).then_inc(x_loaded[1], 16)
            load_ctx(1, 1)
            sp.dma_start(w_raw[:], Wq.rearrange("(c p) n -> p c n", p=P)).then_inc(w_loaded, 16)
            sp.dma_start(wo_raw[:], Wo.rearrange("(c p) n -> p c n", p=P)).then_inc(w_loaded, 16)
            sp.dma_start(wkv_raw[:], Wkv.rearrange("(c p) n -> p c n", p=P)).then_inc(w_loaded, 16)
            for row, w in ((nw_row, norm_w), (nb_row, norm_b), (ow_row, out_norm_w), (ob_row, out_norm_b)):
                sp.dma_start(row[:], w.rearrange("(a d) -> a d", a=1).broadcast_to([P, D])).then_inc(small_loaded, 16)
            sp.dma_start(rw_raw[:], routerT.rearrange("(c p) e -> p c e", p=P)).then_inc(small_loaded, 16)
            with sp.Fori(1, B * NC // 4) as i:
                for s in range(2):
                    sp.wait_ge(ctxT_lo_done, 4 * i + 2 * s - 2)
                    sp.wait_ge(ctxN_lo_done, 4 * i + 2 * s - 2)
                    load_ctx(2 * i + s, s)

            def load_gate_up(q, c, first=False):
                if not first:
                    sp.wait_ge(guT_lo_done, q - 1)
                sp.dma_start(gu_raw[:, c % 2], gate_upT_chunks[bass.ds(q, 1)].rearrange("a p m j f -> p (a m) j f")).then_inc(gu_loaded[c % 2], 16)

            def load_down(e, k, first=False):
                if not first:
                    sp.wait_ge(dnT_lo_done, NF * e + 2 * k - 2)
                sp.dma_start(down_raw[:, 2 * (k % 2):2 * (k % 2) + 2, :],
                             downT_pairs[bass.ds(NF // 2 * e + k, 1)].rearrange("a p c d -> p (a c) d")).then_inc(down_loaded[k % 2], 16)

            gate_upT_chunks = gate_upT.rearrange("e c p m j f -> (e c) p m j f")
            downT_pairs = downT.rearrange("e k p c d -> (e k) p c d")

            sp.wait_ge(proj_done, USES * B)
            for c in range(2):
                load_gate_up(c, c, first=True)
            sp.wait_ge(self_added, NT)
            for k in range(2):
                load_down(0, k, first=True)
            for c in range(2, NF):
                load_gate_up(c, c)
                if c % 2 == 1 and c < NF - 1:
                    load_down(0, (c + 1) // 2)
            with sp.Fori(1, E) as e:
                for c in range(NF):
                    load_gate_up(NF * e + c, c)
                    if c % 2 == 0:
                        load_down(e, c // 2)
            for t in range(NT):
                sp.wait_ge(combined, NT * (E - 1) + t + 1)
                sp.dma_start(out_dram[:, t, :], x_res[:, t, :]).then_inc(stored, 16)
            sp.wait_ge(stored, 16 * NT)

        @block.gpsimd
        def _(pool):
            nc.gpsimd.memset(ident[:], 0.0).then_inc(const_ready, 1)
            nc.gpsimd.memset(neg_half[:], -0.5).then_inc(const_ready, 1)
            for e in range(E):
                nc.gpsimd.memset(rank[:, e:e + 1], float(E - e)).then_inc(const_ready, 1)
            pool.wait_ge(const_ready, 2 + E)
            nc.gpsimd.affine_select(out=ident[:], in_=ident[:], compare_op=ALU.not_equal, fill=1.0,
                                    base=0, pattern=[[-1, P]], channel_multiplier=1).then_inc(const_ready, 1)

            def power(n, b):
                pool.wait_ge(norm_var[n], b + 1)
                tiles = slice(TB * b, TB * b + TB)
                nc.gpsimd.tensor_tensor(rstd[n][:, tiles], var_eps[n][:, tiles], neg_half[:], ALU.pow).then_inc(norm_rstd[n], 1)

            def ctx_lo(g, k):
                pool.wait_ge(ctxN_hi_done, g + 1)
                nc.gpsimd.tensor_tensor(ctxN_lo[:, k % 2, :], ctxN_raw[:, (k // 2) % 2, k % 2, :],
                                        f32(ctxN_hi[:, k % 2, :]), ALU.subtract).then_inc(ctxN_lo_done, 1)

            def weight_lo(k):
                pool.wait_ge(w_hi_done, k + 1)
                raw, hi, lo = ((w_raw, wq_hi, wq_lo), (wo_raw, wo_hi, wo_lo))[k // KD]
                c = k % KD
                nc.gpsimd.tensor_tensor(lo[:, c, :], raw[:, c, :], f32(hi[:, c, :]), ALU.subtract).then_inc(w_lo_done, 1)
                if k == 2 * KD - 1:
                    pool.wait_ge(w_hi_done, 2 * KD + 3)
                    for r in range(2):
                        nc.gpsimd.tensor_tensor(wk2_lo[:, :, r, :], wkv_raw[:, :, 0:DH], f32(wk2_hi[:, :, r, :]),
                                                ALU.subtract).then_inc(w_lo_done, 1)
                    nc.gpsimd.tensor_tensor(wv_lo[:], wkv_raw[:, :, DH:], f32(wv_hi[:]), ALU.subtract).then_inc(w_lo_done, 1)

            power("a", 0)
            ctx_lo(0, 0)
            power("a", 1)
            for g in range(1, 4):
                ctx_lo(g, g)
            with pool.Fori(1, NC // 4) as i:
                for k in range(4):
                    ctx_lo(4 * i + k, k)
            for k in range(9):
                ctx_lo(NC + k, k)
                if k >= 1:
                    weight_lo(k - 1)
                if k == 1:
                    power("b", 0)
                if k == 4:
                    power("b2", 0)
            for k in range(9, 12):
                ctx_lo(NC + k, k)
            with pool.Fori(NC // 4 + 3, B * NC // 4) as i:
                for k in range(4):
                    ctx_lo(4 * i + k, k)

            pool.wait_ge(cross_done, B * NC)
            for w in (vp_hi, vp_lo):
                for side in (0, 2):
                    nc.gpsimd.memset(f32(w[:, :, side, :]), 0.0).then_inc(pads_zero, 1)
            for b in range(B):
                if b == 0:
                    power("b", 1)
                    power("b2", 1)
                else:
                    power("y", 0)
                for u in range(UNITS):
                    v = UNITS * b + u
                    if b == 1 and u == 4:
                        power("c", 0)
                    pool.wait_ge(inv_done, v + 1)
                    p = prob[:, u % 4, :]
                    nc.gpsimd.tensor_tensor(p, p, row_inv[:, v:v + 1].broadcast_to([P, S]), ALU.mult).then_inc(prob_done, 1)
            power("y", 1)
            power("c", 1)

        @block.scalar
        def _(act):
            def xT_hi_tile(n, t, banks):
                act.wait_ge(xn_turned[n], t + 1)
                nc.scalar.activation(xT_hi[:, :, tile_cols(t)], quarters(banks[t % 2]), ACT.Copy).then_inc(xT_hi_done[n], 1)

            for t in range(TB):
                xT_hi_tile("a", t, TURN)

            def ctxT_hi_step(g, k, landed, first=False):
                act.wait_ge(ctxT_loaded[(k // 2) % 2], landed)
                if not first:
                    act.wait_ge(x1_done, g - 1)
                nc.scalar.activation(ctxT_hi[:, k % 2], ctxT_raw[:, (k // 2) % 2, :, tile_cols(k % 2)],
                                     ACT.Copy).then_inc(ctxT_hi_done, 1)

            def gelu_step(g, k, first=False):
                act.wait_ge(x1_done, g + 1)
                if not first:
                    act.wait_ge(hid_done, g - 1)
                nc.scalar.activation(activated[:, k % 2, :], X1[k % 2][:, :], ACT.Gelu_apprx_tanh).then_inc(gelu_done, 1)

            def hid_hi_step(g, k, first=False):
                act.wait_ge(hid_done, g + 1)
                if not first:
                    act.wait_ge(cross_done, g - 1)
                nc.scalar.activation(hidT_hi[:, k % 2, :], hid[:, k % 2, :], ACT.Copy).then_inc(hidT_hi_done, 1)

            def weight_hi(k):
                if k == 0:
                    act.wait_ge(w_loaded, 48)
                raw, hi = ((w_raw, wq_hi), (wo_raw, wo_hi))[k // KD]
                c = k % KD
                nc.scalar.activation(hi[:, c, :], raw[:, c, :], ACT.Copy).then_inc(w_hi_done, 1)
                if k == 2 * KD - 1:
                    for r in range(2):
                        nc.scalar.activation(wk2_hi[:, :, r, :], wkv_raw[:, :, 0:DH], ACT.Copy).then_inc(w_hi_done, 1)
                    nc.scalar.activation(wv_hi[:], wkv_raw[:, :, DH:], ACT.Copy).then_inc(w_hi_done, 1)

            for b in range(B):
                g0, l0, n = b * NC, 16 * (b * NC // 4), HEAD_STEPS[b]
                for k in range(2):
                    ctxT_hi_step(g0 + k, k, l0 + 16, first=(b == 0))
                gelu_step(g0, 0, first=(b == 0))
                hid_hi_step(g0, 0, first=(b == 0))

                def cross_step(g, k, landed, ahead2=True, ahead1=True, first=False):
                    if ahead2:
                        ctxT_hi_step(g + 2, k + 2, landed)
                    if ahead1:
                        gelu_step(g + 1, k + 1, first)
                        hid_hi_step(g + 1, k + 1, first)

                for k in range(n):
                    cross_step(g0 + k, k, l0 + 16 * (1 + (k + 2) // 4), first=(b == 0 and k == 0))
                    if b == 0 and k == 0:
                        for t in range(TB, NT):
                            xT_hi_tile("a", t, TURN)
                    if b == 1:
                        weight_hi(k)
                        if k in (4, 5):
                            for t in (2 * k - 8, 2 * k - 7):
                                xT_hi_tile("b", t, TURN)
                with act.Fori(n // 4, NC // 4 - 1) as i:
                    for k in range(4):
                        cross_step(4 * i + (g0 + k), k, 16 * i + (l0 + 16 * (1 + (k + 2) // 4)))
                for k in range(4):
                    cross_step(g0 + NC - 4 + k, k, l0 + 4 * NC, ahead2=k < 2, ahead1=k < 3)

            act.wait_ge(cross_done, B * NC)
            nc.scalar.activation(rw_hi[:], rw_raw[:], ACT.Copy).then_inc(rw_hi_done, 1)
            for b in range(B):
                def from_bank(m):
                    act.wait_ge(proj_done, USES * b + m + 1)
                    return PROJ[(USES * b + m) % 2]

                nc.scalar.activation(kT_hi[:], from_bank(0)[:, :], ACT.Copy).then_inc(proj_hi_done, 1)
                for t in range(TB):
                    nc.scalar.activation(vp_hi[:, t, 1, :], from_bank(1 + t)[:, 0:DH], ACT.Copy).then_inc(proj_hi_done, 1)
                if b == 1:
                    act.wait_ge(y_done, TB)
                for p in range(PAIRS):
                    ps = from_bank(1 + TB + p)
                    for r, half in enumerate((slice(0, DH), slice(DH, P))):
                        nc.scalar.activation(q_o[half, p, r, :], ps[half, :], ACT.Copy, scale=SCALE).then_inc(proj_hi_done, 1)

                for u in range(PIPE):
                    v = UNITS * b + u
                    if 0 <= u - TURN_LAG < UNITS:
                        w, i, h = v - TURN_LAG, (u - TURN_LAG) % TB, (u - TURN_LAG) // TB
                        act.wait_ge(prob_turned, w + 1)
                        if HEADS * b + h >= 2:
                            act.wait_ge(pv_done, HEADS * b + h - 1)
                        nc.scalar.activation(probT_hi[:, h % 2, :, tile_cols(i)], quarters(TURN[w % 2]),
                                             ACT.Copy).then_inc(probT_hi_done, 1)
                    if u < UNITS:
                        act.wait_ge(max_done, v + 1)
                        if v >= 4:
                            act.wait_ge(prob_turned, v - 3)
                        nc.scalar.activation(prob[:, u % 4, :], SIM[u % 2][:, :], ACT.Exp,
                                             bias=neg_max[:, v:v + 1], accum_out=row_sum[:, v:v + 1]).then_inc(exp_done, 1)
                    t = behind(u, BEHIND[b] + 2)
                    if t is not None:
                        xT_hi_tile("bc"[b], (TB, 0)[b] + t, PROJ)
                    p = pair_out(u)
                    if p is not None:
                        act.wait_ge(pv_done, HEADS * b + 2 * p + 2)
                        nc.scalar.activation(q_o[:, p, 0, :], HEAD_OUT[p % 2][:, :], ACT.Copy).then_inc(oT_hi_done, 1)
                    if b == 1 and u == UNITS:
                        for c in range(2):
                            act.wait_ge(gu_loaded[c], 16)
                            nc.scalar.activation(guT_hi[:, c], gu_raw[:, c], ACT.Copy).then_inc(guT_hi_done, 1)

            def guT_hi_step(c, q, landed, free):
                act.wait_ge(gu_loaded[c % 2], landed)
                act.wait_ge(up_done, free)
                nc.scalar.activation(guT_hi[:, c % 2], gu_raw[:, c % 2], ACT.Copy).then_inc(guT_hi_done, 1)

            def dnT_hi_step(e, c, landed, first):
                act.wait_ge(down_loaded[(c // 2) % 2], landed)
                if not first:
                    act.wait_ge(down_done, NT * e)
                nc.scalar.activation(dnT_hi[:, c, :], down_raw[:, c % 4, :], ACT.Copy).then_inc(dnT_hi_done, 1)

            def silu_step(n, v, first):
                act.wait_ge(gate_done, v + 1)
                if not first:
                    act.wait_ge(act_done, v - 1)
                nc.scalar.activation(activated[:, n % 2, :], GATE[n % 2][:, :], ACT.Silu).then_inc(silu_done, 1)

            def hT_hi_step(c, s, n, v):
                act.wait_ge(act_done, v + 1)
                nc.scalar.activation(hT_hi[:, c, s * S:(s + 1) * S], hid[:, n % 2, :], ACT.Copy).then_inc(hT_hi_done, 1)

            def expert(e, first, last):
                for n, (c, s) in enumerate(hidden_order(first)):
                    v = 2 * NF * e + n
                    silu_step(n, v, first and n < 2)
                    hT_hi_step(c, s, n, v)
                    if first and n == 1:
                        for t in range(TB, NT):
                            xT_hi_tile("c", t, TURN)
                    if first and n == 3:
                        act.wait_ge(route_gap, 1)
                        nc.scalar.activation(r_exp[:], r_gap[:], ACT.Exp, scale=-1.0).then_inc(route_exp, 1)
                    if n % 2 == 1:
                        dnT_hi_step(e, n // 2, 32 * e + 16 * (n // 8 + 1), first)
                        if not (last and n // 2 + 2 >= NF):
                            guT_hi_step(n // 2 + 2, NF * e + n // 2 + 2, 64 * e + 16 * ((n // 2 + 2) // 2 + 1),
                                        v + (2 if first and n == 1 else 1))

            expert(0, True, False)
            with act.Fori(1, E - 1) as e:
                expert(e, False, False)
            expert(E - 1, False, True)

        @block.vector
        def _(dve):
            V = nc.vector

            def stat_tile(n, src, t):
                V.bn_stats(stats[n][:, t, :], src).then_inc(norm_stat[n], 1)

            def stat_end(n, b):
                dve.wait_ge(norm_stat[n], 2 * TB * b + TB)
                for t in range(TB * b, TB * b + TB):
                    V.bn_aggr(mv[n][:, t, :], stats[n][:, t, :]).then_inc(norm_stat[n], 1)
                dve.wait_ge(norm_stat[n], 2 * TB * (b + 1))
                tiles = slice(TB * b, TB * b + TB)
                V.tensor_scalar_add(var_eps[n][:, tiles], mv[n][:, tiles, 1], EPS).then_inc(norm_var[n], 1)

            def norm_tile(n, t, done):
                V.tensor_scalar(xn[:, t % TB, :], x_res[:, t, :], mv[n][:, t, 0:1], rstd[n][:, t:t + 1],
                                ALU.subtract, ALU.mult).then_inc(done, 1)

            def xT_lo_tile(n, t, banks):
                dve.wait_ge(xT_hi_done[n], t + 1)
                V.tensor_tensor(xT_lo[:, :, tile_cols(t)], quarters(banks[t % 2]), f32(xT_hi[:, :, tile_cols(t)]),
                                ALU.subtract).then_inc(xT_lo_done[n], 1)

            def whole_norm(n, b):
                for t in range(TB * b, TB * b + TB):
                    stat_tile(n, x_res[:, t, :], t)
                stat_end(n, b)
                dve.wait_ge(norm_rstd[n], b + 1)
                dve.wait_ge(xn_turned[n], TB * b) if b else None
                for t in range(TB * b, TB * b + TB):
                    norm_tile(n, t, xn_ready[n])
                    if t % TB >= 1:
                        xT_lo_tile(n, t - 1, TURN)
                xT_lo_tile(n, TB * b + TB - 1, TURN)

            def b_first(b, t):
                norm_tile("b", TB * b + t, b_plain)

            def b_second_stat(b, t):
                dve.wait_ge(b_plain, TB * b + t + 1)
                stat_tile("b2", xn[:, t, :], TB * b + t)

            def b_scale(b, t):
                i = TB * b + t
                V.scalar_tensor_tensor(xn[:, t, :], xn[:, t, :], mv["b2"][:, i, 0:1], nw_row[:],
                                       ALU.subtract, ALU.mult).then_inc(b_scaled, 1)

            def b_last(b, t):
                i = TB * b + t
                dve.wait_ge(b_scaled, i + 1)
                V.scalar_tensor_tensor(xn[:, t, :], xn[:, t, :], rstd["b2"][:, i:i + 1], nb_row[:],
                                       ALU.mult, ALU.add).then_inc(xn_ready["b"], 1)

            dve.wait_ge(x_loaded[0], 16)
            whole_norm("a", 0)

            def ctxT_lo_step(g, k):
                dve.wait_ge(ctxT_hi_done, g + 1)
                V.tensor_tensor(ctxT_lo[:, k % 2], ctxT_raw[:, (k // 2) % 2, :, tile_cols(k % 2)], f32(ctxT_hi[:, k % 2]),
                                ALU.subtract).then_inc(ctxT_lo_done, 1)

            def ctxN_hi_step(g, k, landed, first=False):
                dve.wait_ge(ctxN_loaded[(k // 2) % 2], landed)
                if not first:
                    dve.wait_ge(cross_done, g - 1)
                V.tensor_copy(ctxN_hi[:, k % 2, :], ctxN_raw[:, (k // 2) % 2, k % 2, :]).then_inc(ctxN_hi_done, 1)

            def hid_step(g, k, first=False):
                dve.wait_ge(gelu_done, g + 1)
                if not first:
                    dve.wait_ge(hidT_lo_done, g - 1)
                V.tensor_tensor(hid[:, k % 2, :], X1[k % 2][:, :], activated[:, k % 2, :], ALU.mult).then_inc(hid_done, 1)

            def hid_lo_step(g, k):
                dve.wait_ge(hidT_hi_done, g + 1)
                V.tensor_tensor(hidT_lo[:, k % 2, :], hid[:, k % 2, :], f32(hidT_hi[:, k % 2, :]),
                                ALU.subtract).then_inc(hidT_lo_done, 1)

            def b_norm_part(k):
                if k == 0:
                    dve.wait_ge(cross_added, TB)
                    for t in range(TB):
                        stat_tile("b", x_res[:, t, :], t)
                    stat_end("b", 0)
                elif k == 1:
                    dve.wait_ge(norm_rstd["b"], 1)
                    for t in range(TB):
                        b_first(0, t)
                elif k == 2:
                    for t in range(TB):
                        b_second_stat(0, t)
                    stat_end("b2", 0)
                elif k == 3:
                    dve.wait_ge(small_loaded, 16 * 5)
                    for t in range(TB):
                        b_scale(0, t)
                elif k == 4:
                    dve.wait_ge(norm_rstd["b2"], 1)
                    for t in range(2):
                        b_last(0, t)
                elif k == 5:
                    for t in range(2, TB):
                        b_last(0, t)
                        xT_lo_tile("b", t - 2, TURN)
                elif k == 6:
                    for t in range(2, TB):
                        xT_lo_tile("b", t, TURN)

            for b in range(B):
                g0, l0, n = b * NC, 16 * (b * NC // 4), HEAD_STEPS[b]
                for k in range(2):
                    ctxT_lo_step(g0 + k, k)
                ctxN_hi_step(g0, 0, l0 + 16, first=(b == 0))
                hid_step(g0, 0, first=(b == 0))
                hid_lo_step(g0, 0)

                def cross_step(g, k, landed, ahead2=True, ahead1=True, first=False):
                    if ahead2:
                        ctxT_lo_step(g + 2, k + 2)
                    if ahead1:
                        ctxN_hi_step(g + 1, k + 1, landed, first)
                        hid_step(g + 1, k + 1, first)
                        hid_lo_step(g + 1, k + 1)

                if b == 1:
                    dve.wait_ge(cross_done, NC)
                    for t in range(TB):
                        xt = x_res[:, t, :]
                        V.tensor_tensor(xt, ACC[t][:, :], xt, ALU.add).then_inc(cross_added, 1)
                for k in range(n):
                    cross_step(g0 + k, k, l0 + 16 * (1 + (k + 1) // 4), first=(b == 0 and k == 0))
                    if b == 0 and k == 0:
                        dve.wait_ge(x_loaded[1], 16)
                        whole_norm("a", 1)
                    if b == 1:
                        b_norm_part(k)
                with dve.Fori(n // 4, NC // 4 - 1) as i:
                    for k in range(4):
                        cross_step(4 * i + (g0 + k), k, 16 * i + (l0 + 16 * (1 + (k + 1) // 4)))
                for k in range(4):
                    cross_step(g0 + NC - 4 + k, k, l0 + 4 * NC, ahead2=k < 2, ahead1=k < 3)
            dve.wait_ge(cross_done, B * NC)
            for t in (*range(NT - 2, NT), *range(TB, NT - 2)):
                xt = x_res[:, t, :]
                V.tensor_tensor(xt, ACC[t - TB][:, :], xt, ALU.add).then_inc(cross_added, 1)

            def y_norm(b, part):
                tiles = range(TB * b, TB * b + TB)
                if part == 0:
                    for t in tiles:
                        dve.wait_ge(y_done, t + 1)
                        stat_tile("y", Y_OF[b][t % TB][:, :], t)
                    stat_end("y", b)
                    for t in tiles:
                        V.scalar_tensor_tensor(y_sb[:, t % TB, :], Y_OF[b][t % TB][:, :], mv["y"][:, t, 0:1], ow_row[:],
                                               ALU.subtract, ALU.mult).then_inc(y_scaled, 1)
                else:
                    dve.wait_ge(norm_rstd["y"], b + 1)
                    for t in tiles:
                        dve.wait_ge(y_scaled, t + 1)
                        V.scalar_tensor_tensor(y_sb[:, t % TB, :], y_sb[:, t % TB, :], rstd["y"][:, t:t + 1], ob_row[:],
                                               ALU.mult, ALU.add).then_inc(y_normed, 1)
                    for t in tiles:
                        xt = x_res[:, t, :]
                        dve.wait_ge(y_normed, t + 1)
                        V.tensor_tensor(xt, xt, y_sb[:, t % TB, :], ALU.add).then_inc(self_added, 1)

            for b in range(B):
                his = (1 + TB + 2 * PAIRS) * b
                dve.wait_ge(proj_hi_done, his + 1)
                V.tensor_tensor(kT_lo[:], PROJ[USES * b % 2][:, :], f32(kT_hi[:]), ALU.subtract).then_inc(proj_lo_done, 1)
                for t in range(TB):
                    dve.wait_ge(proj_hi_done, his + 2 + t)
                    V.tensor_tensor(vp_lo[:, t, 1, :], PROJ[(USES * b + 1 + t) % 2][:, 0:DH],
                                    f32(vp_hi[:, t, 1, :]), ALU.subtract).then_inc(proj_lo_done, 1)
                if b == 1:
                    y_norm(0, 0)
                for p in range(PAIRS):
                    if b == 0:
                        if p == 0:
                            dve.wait_ge(cross_added, NT)
                            for t in range(TB, NT):
                                stat_tile("b", x_res[:, t, :], t)
                            stat_end("b", 1)
                        elif p == 1:
                            dve.wait_ge(norm_rstd["b"], 2)
                            dve.wait_ge(xn_turned["b"], TB)
                            for t in range(TB):
                                b_first(1, t)
                        elif p == 2:
                            for t in range(TB):
                                b_second_stat(1, t)
                            stat_end("b2", 1)
                    elif p == 1:
                        y_norm(0, 1)
                    ps = PROJ[(USES * b + 1 + TB + p) % 2]
                    dve.wait_ge(proj_hi_done, his + 1 + TB + 2 * p + 2)
                    for r, (own, other) in enumerate(((slice(0, DH), slice(DH, P)), (slice(DH, P), slice(0, DH)))):
                        V.scalar_tensor_tensor(q_o[other, p, r, :], ps[own, :], SCALE, f32(q_o[own, p, r, :]),
                                               ALU.mult, ALU.subtract).then_inc(proj_lo_done, 1)
                if b == 0:
                    for t in range(TB):
                        b_scale(1, t)
                    dve.wait_ge(norm_rstd["b2"], 2)

                for u in range(PIPE):
                    v = UNITS * b + u
                    if 0 <= u - LO_LAG < UNITS:
                        w, i, h = v - LO_LAG, (u - LO_LAG) % TB, (u - LO_LAG) // TB
                        dve.wait_ge(probT_hi_done, w + 1)
                        V.tensor_tensor(probT_lo[:, h % 2, :, tile_cols(i)], quarters(TURN[w % 2]),
                                        f32(probT_hi[:, h % 2, :, tile_cols(i)]), ALU.subtract).then_inc(probT_lo_done, 1)
                    if u < UNITS:
                        dve.wait_ge(sim_done, v + 1)
                        V.tensor_reduce(neg_max[:, v:v + 1], SIM[u % 2][:, :], AX_X, ALU.max, negate=True).then_inc(max_done, 1)
                    if 0 <= u - 1 < UNITS:
                        dve.wait_ge(exp_done, v)
                        V.reciprocal(row_inv[:, v - 1:v], row_sum[:, v - 1:v]).then_inc(inv_done, 1)
                    if b == 1 and u < TB:
                        if u == 0:
                            dve.wait_ge(self_added, TB)
                        stat_tile("c", x_res[:, u, :], u)
                    if b == 1 and u == TB:
                        stat_end("c", 0)
                    t = behind(u, BEHIND[b])
                    if t is not None and b == 0:
                        b_last(1, t)
                    if t is not None and b == 1:
                        if t == 0:
                            dve.wait_ge(norm_rstd["c"], 1)
                            dve.wait_ge(xn_turned["b"], NT)
                        norm_tile("c", t, xn_ready["c"])
                    t = behind(u, BEHIND[b] + 3)
                    if t is not None:
                        xT_lo_tile("bc"[b], (TB, 0)[b] + t, PROJ)
                    p = pair_out(u)
                    if p is not None:
                        dve.wait_ge(oT_hi_done, PAIRS * b + p + 1)
                        V.tensor_tensor(q_o[:, p, 1, :], HEAD_OUT[p % 2][:, :], f32(q_o[:, p, 0, :]),
                                        ALU.subtract).then_inc(oT_lo_done, 1)
                    if b == 1 and u == UNITS:
                        for c in range(2):
                            dve.wait_ge(guT_hi_done, c + 1)
                            V.tensor_tensor(guT_lo[:, c], gu_raw[:, c], f32(guT_hi[:, c]), ALU.subtract).then_inc(guT_lo_done, 1)
                        dve.wait_ge(rw_hi_done, 1)
                        V.tensor_tensor(rw_lo[:], rw_raw[:], f32(rw_hi[:]), ALU.subtract).then_inc(rw_lo_done, 1)
            y_norm(1, 0)
            y_norm(1, 1)

            def over_experts(ap):
                return ap.unsqueeze(2).broadcast_to([P, NT, E])

            def route():
                step = [0]

                def then(ins):
                    step[0] += 1
                    ins.then_inc(route_step, 1)
                    dve.wait_ge(route_step, step[0])

                first, second = 0, 1
                magnitude, limit, cand, others, rest = r_tmp
                ranks = rank[:].unsqueeze(1).broadcast_to([P, NT, E])
                dve.wait_ge(logits_done, NT)
                then(V.tensor_copy(logit[:], TURN[1][:, 0:NT * E].rearrange("p (t e) -> p t e", e=E)))
                then(V.scalar_tensor_tensor(magnitude[:], logit[:], -1.0, logit[:], ALU.mult, ALU.max))
                for n, score in ((first, logit), (second, rest)):
                    top_b = over_experts(r_top[:, n, :])
                    then(V.tensor_reduce(r_top[:, n, :], score[:], AX_X, ALU.max))
                    then(V.tensor_tensor(cand[:], score[:], top_b, ALU.is_ge))
                    then(V.tensor_tensor(cand[:], cand[:], ranks, ALU.mult))
                    then(V.tensor_reduce(r_red[:, n, :], cand[:], AX_X, ALU.max))
                    then(V.tensor_tensor(r_hot[:, n], cand[:], over_experts(r_red[:, n, :]), ALU.is_equal))
                    then(V.tensor_tensor(r_gap[:, n], top_b, logit[:], ALU.subtract))
                    then(V.tensor_tensor(limit[:], magnitude[:], top_b, ALU.max))
                    then(V.scalar_tensor_tensor(r_keep[:, n], limit[:], JITTER, r_gap[:, n], ALU.mult, ALU.is_ge))
                    if n == first:
                        then(V.tensor_scalar(others[:], r_hot[:, n], -1.0, 1.0, ALU.mult, ALU.add))
                        then(V.tensor_tensor(rest[:], logit[:], others[:], ALU.mult))
                        then(V.scalar_tensor_tensor(rest[:], r_hot[:, n], LOWEST, rest[:], ALU.mult, ALU.add))
                then(V.tensor_tensor(r_keep[:, second], r_keep[:, second], others[:], ALU.mult))
                V.tensor_scalar_max(r_gap[:, second], r_gap[:, second], 0.0).then_inc(route_gap, 1)
                dve.wait_ge(route_exp, 1)
                then(V.tensor_tensor(r_keep[:], r_keep[:], r_exp[:], ALU.mult))
                then(V.tensor_reduce(r_sum[:], r_keep[:], AX_X, ALU.add))
                then(V.reciprocal(r_mult[:], r_sum[:]))
                for n in (first, second):
                    then(V.tensor_tensor(r_hot[:, n], r_hot[:, n], over_experts(r_mult[:, n, :]), ALU.mult))
                then(V.tensor_tensor(dense_w[:], r_hot[:, first], r_hot[:, second], ALU.add))

            def hidden_step(c, s, n, v, first):
                dve.wait_ge(silu_done, v + 1)
                dve.wait_ge(up_done, v + 1)
                if not first:
                    dve.wait_ge(hT_lo_done, v - 1)
                V.tensor_tensor(hid[:, n % 2, :], UP[n % 2][:, :], activated[:, n % 2, :], ALU.mult).then_inc(act_done, 1)
                dve.wait_ge(hT_hi_done, v + 1)
                V.tensor_tensor(hT_lo[:, c, s * S:(s + 1) * S], hid[:, n % 2, :],
                                f32(hT_hi[:, c, s * S:(s + 1) * S]), ALU.subtract).then_inc(hT_lo_done, 1)

            def expert(e, first, last):
                for n, (c, s) in enumerate(hidden_order(first)):
                    v = 2 * NF * e + n
                    hidden_step(c, s, n, v, first and n < 2)
                    if first and n == 1:
                        whole_norm("c", 1)
                    if first and n == 3:
                        route()
                    if n % 2 == 1:
                        c = n // 2
                        dve.wait_ge(dnT_hi_done, NF * e + c + 1)
                        V.tensor_tensor(dnT_lo[:, c, :], down_raw[:, c % 4, :], f32(dnT_hi[:, c, :]),
                                        ALU.subtract).then_inc(dnT_lo_done, 1)
                        if not (last and c + 2 >= NF):
                            dve.wait_ge(guT_hi_done, NF * e + c + 3)
                            V.tensor_tensor(guT_lo[:, c % 2], gu_raw[:, c % 2], f32(guT_hi[:, c % 2]),
                                            ALU.subtract).then_inc(guT_lo_done, 1)
                if not first:
                    dve.wait_ge(combined, NT * e)
                V.tensor_copy(expert_w[:].unsqueeze(2), dense_w[:, :, bass.ds(e, 1)]).then_inc(weight_picked, 1)
                dve.wait_ge(weight_picked, e + 1)
                for t in range(NT):
                    dve.wait_ge(down_done, NT * e + (t + 1))
                    xt = x_res[:, t, :]
                    V.scalar_tensor_tensor(xt, DOWN_OUT[t % 2][:, :], expert_w[:, t:t + 1], xt,
                                           ALU.mult, ALU.add).then_inc(combined, 1)

            expert(0, True, False)
            with dve.Fori(1, E - 1) as e:
                expert(e, False, False)
            expert(E - 1, False, True)

        @block.tensor
        def _(pe):
            def product(out_ap, pairs, start=True, stop=True):
                n = len(pairs)
                for i, ((l_hi, l_lo), (r_hi, r_lo)) in enumerate(pairs):
                    nc.tensor.matmul(out_ap, l_lo, r_hi, start=start and i == 0, stop=False)
                    nc.tensor.matmul(out_ap, l_hi, r_lo, start=False, stop=False)
                    last = nc.tensor.matmul(out_ap, l_hi, r_hi, start=False, stop=stop and i == n - 1)
                return last

            def turn(dst, src):
                for i in range(4):
                    last = nc.tensor.transpose(dst[:, tile_cols(i)], src[:, tile_cols(i)], ident[:])
                return last

            def xn_turn(n, t, banks):
                pe.wait_ge(xn_ready[n], t + 1)
                if t >= 2:
                    pe.wait_ge(xT_lo_done[n], t - 1)
                turn(banks[t % 2], xn[:, t % TB, :]).then_inc(xn_turned[n], 1)

            def xT_cols(c, lo, n):
                return xT_hi[:, c, lo:lo + n], xT_lo[:, c, lo:lo + n]

            pe.wait_ge(const_ready, 3 + E)
            for t in range(TB):
                xn_turn("a", t, TURN)
            pe.wait_ge(xT_lo_done["a"], TB)

            def x1_step(b, g, k, first=False):
                pe.wait_ge(ctxT_lo_done, g + 1)
                if not first:
                    pe.wait_ge(hid_done, g - 1)
                product(X1[k % 2][:, :],
                        [((ctxT_hi[:, k % 2, c, :], ctxT_lo[:, k % 2, c, :]), xT_cols(c, b * S, S))
                         for c in range(KD)]).then_inc(x1_done, 1)

            def cross_out(g, k, start, stop):
                pe.wait_ge(hidT_lo_done, g + 1)
                pe.wait_ge(ctxN_lo_done, g + 1)
                for t in range(TB):
                    last = product(ACC[t][:, :],
                                   [((hidT_hi[:, k % 2, tile_cols(t)], hidT_lo[:, k % 2, tile_cols(t)]),
                                     (ctxN_hi[:, k % 2, :], ctxN_lo[:, k % 2, :]))], start=start, stop=stop)
                last.then_inc(cross_done, 1)

            for b in range(B):
                g0, n = b * NC, HEAD_STEPS[b]
                x1_step(b, g0, 0, first=(b == 0))
                if b == 1:
                    x1_step(b, g0 + 1, 1)
                    pe.wait_ge(cross_added, TB)

                def cross_step(g, k, ahead1=True, start=False, stop=False, first=False):
                    if ahead1:
                        x1_step(b, g + 1, k + 1, first)
                    cross_out(g, k, start, stop)

                for k in range(n):
                    cross_step(g0 + k, k, ahead1=not (b == 1 and k == 0), start=(k == 0), first=(b == 0 and k == 0))
                    if b == 0 and k == 0:
                        for t in range(TB, NT):
                            xn_turn("a", t, TURN)
                    if b == 1 and k in (4, 5):
                        for t in (2 * k - 8, 2 * k - 7):
                            xn_turn("b", t, TURN)
                with pe.Fori(n // 4, NC // 4 - 1) as i:
                    for k in range(4):
                        cross_step(4 * i + (g0 + k), k)
                for k in range(4):
                    cross_step(g0 + NC - 4 + k, k, ahead1=k < 3, stop=(k == 3))
                if b == 0:
                    pe.wait_ge(xT_lo_done["a"], NT)

            pe.wait_ge(pads_zero, 4)
            pe.wait_ge(w_lo_done, 2 * KD + 3)
            pe.wait_ge(cross_added, TB + 2)

            def bank_for(b, m):
                n = USES * b + m
                if n >= 2:
                    prev = n - 2
                    per = 1 + TB + 2 * PAIRS
                    pb, pm = prev // USES, prev % USES
                    pe.wait_ge(proj_lo_done, per * pb + (pm + 1 if pm <= TB else 1 + TB + 2 * (pm - TB)))
                return PROJ[n % 2]

            def k_and_v(b):
                pe.wait_ge(xT_lo_done["b"], TB * (b + 1))
                product(bank_for(b, 0)[:, :],
                        [((wk2_hi[:, c].rearrange("p r d -> p (r d)"), wk2_lo[:, c].rearrange("p r d -> p (r d)")),
                          xT_cols(c, b * S, S)) for c in range(KD)]).then_inc(proj_done, 1)
                for t in range(TB):
                    product(bank_for(b, 1 + t)[:, 0:DH],
                            [(xT_cols(c, b * S + t * P, P), (wv_hi[:, c, :], wv_lo[:, c, :]))
                             for c in range(KD)]).then_inc(proj_done, 1)

            def y_tiles(b):
                pe.wait_ge(oT_lo_done, PAIRS * (b + 1))
                for t in range(TB):
                    product(Y_OF[b][t][:, :],
                            [((q_o[:, p, 0, tile_cols(t)], q_o[:, p, 1, tile_cols(t)]), (wo_hi[:, p, :], wo_lo[:, p, :]))
                             for p in range(PAIRS)]).then_inc(y_done, 1)

            for b in range(B):
                k_and_v(b)
                if b == 1:
                    y_tiles(0)
                for p in range(PAIRS):
                    product(bank_for(b, 1 + TB + p)[:, :],
                            [((wq_hi[:, c, tile_cols(p)], wq_lo[:, c, tile_cols(p)]), xT_cols(c, b * S, S))
                             for c in range(KD)]).then_inc(proj_done, 1)
                pe.wait_ge(proj_lo_done, (1 + TB + 2 * PAIRS) * (b + 1))
                if b == 1:
                    pe.wait_ge(y_scaled, TB)

                for u in range(PIPE):
                    v = UNITS * b + u
                    if u < UNITS:
                        h, i = u // TB, u % TB
                        if v >= 2:
                            pe.wait_ge(exp_done, v - 1)
                        q = q_o[:, h // 2, h % 2, tile_cols(i)]
                        nc.tensor.matmul(SIM[u % 2][:, :], q, kT_lo[:], start=True, stop=False)
                        nc.tensor.matmul(SIM[u % 2][:, :], q, kT_hi[:], start=False, stop=True).then_inc(sim_done, 1)
                    if 0 <= u - PV_LAG - TB + 1 < UNITS:
                        h, j = (u - PV_LAG - TB + 1) // TB, (u - PV_LAG - TB + 1) % TB
                        if j == 0:
                            pe.wait_ge(probT_lo_done, TB * (HEADS * b + h + 1))
                            n = PAIRS * b + h // 2
                            if h % 2 == 0 and n >= 2:
                                pe.wait_ge(oT_lo_done, n - 1)
                        pad = slice(1, 3) if h % 2 == 0 else slice(0, 2)
                        last = product(HEAD_OUT[(h // 2) % 2][:, :],
                                       [((vp_hi[:, j, pad].rearrange("p a d -> p (a d)"),
                                          vp_lo[:, j, pad].rearrange("p a d -> p (a d)")),
                                         (probT_hi[:, h % 2, j, :], probT_lo[:, h % 2, j, :]))],
                                       start=h % 2 == 0 and j == 0, stop=h % 2 == 1 and j == TB - 1)
                        if j == TB - 1:
                            last.then_inc(pv_done, 1)
                    if 0 <= u - TURN_LAG < UNITS:
                        w = v - TURN_LAG
                        pe.wait_ge(prob_done, w + 1)
                        if w >= 2:
                            pe.wait_ge(probT_lo_done, w - 1)
                        turn(TURN[w % 2], prob[:, w % 4, :]).then_inc(prob_turned, 1)
                    t = behind(u, BEHIND[b] + 1)
                    if t is not None:
                        xn_turn("bc"[b], (TB, 0)[b] + t, PROJ)

            def hidden(e, n, c, s, first):
                v = 2 * NF * e + n
                if not (first and n < 2):
                    pe.wait_ge(act_done, v - 1)
                for kind, bank_of, done in ((0, GATE, gate_done), (1, UP, up_done)):
                    product(bank_of[n % 2][:, :],
                            [((guT_hi[:, c % 2, kind, j, :], guT_lo[:, c % 2, kind, j, :]), xT_cols(j, s * S, S))
                             for j in range(KD)]).then_inc(done, 1)

            def expert(e, first, last):
                for n, (c, s) in enumerate(hidden_order(first)):
                    if n % 2 == 0 and not first:
                        pe.wait_ge(guT_lo_done, NF * e + c + 1)
                    if first and n >= 4 and n % 2 == 0:
                        pe.wait_ge(guT_lo_done, c + 1)
                    if first and n == 0:
                        pe.wait_ge(guT_lo_done, 2)
                        pe.wait_ge(xT_lo_done["c"], TB)
                    if first and n == 1:
                        y_tiles(1)
                    if first and n == 2:
                        pe.wait_ge(y_scaled, NT)
                        for t in range(TB, NT):
                            xn_turn("c", t, TURN)
                        pe.wait_ge(xT_lo_done["c"], NT)
                        pe.wait_ge(rw_lo_done, 1)
                        for t in range(NT):
                            product(TURN[1][:, t * E:(t + 1) * E],
                                    [(xT_cols(j, t * P, P), (rw_hi[:, j, :], rw_lo[:, j, :]))
                                     for j in range(KD)]).then_inc(logits_done, 1)
                    hidden(e, n, c, s, first)
                for t in range(NT):
                    if t == 0:
                        pe.wait_ge(dnT_lo_done, NF * e + NF)
                        pe.wait_ge(hT_lo_done, 2 * (NF * e + NF) - 1)
                    if t == TB:
                        pe.wait_ge(hT_lo_done, 2 * (NF * e + NF))
                    if not (first and t < 2):
                        pe.wait_ge(combined, NT * e + (t - 1))
                    product(DOWN_OUT[t % 2][:, :],
                            [((hT_hi[:, c, tile_cols(t)], hT_lo[:, c, tile_cols(t)]), (dnT_hi[:, c, :], dnT_lo[:, c, :]))
                             for c in range(NF)]).then_inc(down_done, 1)

            expert(0, True, False)
            with pe.Fori(1, E - 1) as e:
                expert(e, False, False)
            expert(E - 1, False, True)


def kernel(**inputs):
    import numpy as _np
    import concourse.bacc as _bacc
    from concourse import mybir as _mybir
    from concourse.bass_utils import run_bass_kernel_spmd as _run

    given = {k.replace("L0_attn_", "").replace("L0_ffn_", ""): v for k, v in inputs.items()}
    ctx = given["ctx_1024"]
    b, length, d = ctx.shape
    e, f, _ = given["w_gate"].shape
    laid = {
        "x": given["x"],
        "ctx_rows": ctx,
        "ctx_turned": ctx.reshape(b * length // 256, 256, d // 128, 128).transpose(0, 3, 2, 1),
        "Wq": given["Wq"], "Wkv": given["Wkv"], "Wo": given["Wo"],
        "norm_w": given["norm_w"], "norm_b": given["norm_b"],
        "out_norm_w": given["out_norm_w"], "out_norm_b": given["out_norm_b"],
        "router_turned": given["router_w"].T,
        "gate_up": _np.stack([given["w_gate"].reshape(e, f // 128, 128, d // 128, 128),
                              given["w_up"].reshape(e, f // 128, 128, d // 128, 128)]).transpose(1, 2, 5, 0, 4, 3),
        "down": given["w_down"].reshape(e, d, f // 256, 2, 128).transpose(0, 2, 4, 3, 1),
    }
    nc = _bacc.Bacc("TRN2", target_bir_lowering=False, num_devices=1)
    arrays, args = {}, []
    for name, a in laid.items():
        a = _np.ascontiguousarray(a)
        arrays[f"in_{name}"] = a
        args.append(nc.dram_tensor(f"in_{name}", a.shape, _mybir.dt.from_np(a.dtype), kind="ExternalInput").ap())
    out = nc.dram_tensor("out_x", given["x"].shape, F32, kind="ExternalOutput").ap()
    build(nc, *args, out)
    r = _run(nc, [arrays], core_ids=[0])
    return r.results[0]["out_x"]
```

```python
from contextlib import ExitStack

import concourse.bass as bass
from concourse import mybir

F32 = mybir.dt.float32
F32R = mybir.dt.float32r
ALU = mybir.AluOpType
ACT = mybir.ActivationFunctionType
AX_X = mybir.AxisListType.X

P = 128
EPS = 1e-5
JITTER = 2.0 * 0.01
LOWEST = -3.0e38


def build(nc, x, ctxN_in, ctxT_in, Wq, Wkv, Wo, norm_w, norm_b, out_norm_w, out_norm_b, routerT, gate_upT, downT, out):
    B, S, D = x.shape
    L = ctxN_in.shape[1]
    E, NF = gate_upT.shape[:2]
    DH = Wkv.shape[1] // 2
    HEADS = Wq.shape[1] // DH
    SCALE = float(DH) ** -0.5
    KD = D // P
    NT = B * S // P
    TB = NT // B
    NC = L // P
    T = B * S
    PAIRS = HEADS // 2
    UNITS = HEADS * TB
    assert B == 2 and D == 512 and S == 512 and DH == 64 and KD == TB and NC % 4 == 0 and NF == 8
    SLOTS = 5
    HEAD_STEPS = 12

    x_dram = x.rearrange("b (t p) d -> p (b t) d", p=P)
    out_dram = out.rearrange("b (t p) d -> p (b t) d", p=P)
    ctxN_pairs = ctxN_in.rearrange("b (j u p) d -> (b j) p u d", u=2, p=P)

    with ExitStack() as top:
        def sem(name):
            return top.enter_context(nc.semaphore(name))

        def sb(scope, name, shape, dt=F32):
            return scope.enter_context(nc.sbuf_tensor(name, shape, dt))

        def split_sb(scope, name, shape):
            return sb(scope, name + "_hi", shape, F32R), sb(scope, name + "_lo", shape, F32R)

        bank = [top.enter_context(nc.psum_tensor(f"bank{i}", [P, 512], F32)) for i in range(8)]
        TURN = bank[0:2]
        X1, ACC = bank[2:4], bank[4:8]
        SIM, HEAD_OUT = bank[2:4] + bank[6:7], bank[4:6]
        K_BANK, V_BANK = (bank[0], bank[7]), (bank[1], bank[6])
        Q_BANK = ((bank[2], bank[4], bank[5], bank[7]), (bank[7], bank[4], bank[5], bank[7]))
        NORM_BANKS = ((bank[7], bank[5], bank[7], bank[6]), (bank[2], bank[3], bank[4], bank[2]))
        Y_OF = (bank[2:4] + bank[0:2], bank[0:2] + bank[6:8])
        GATE, UP, DOWN_OUT = bank[2:4], bank[4:6], bank[6:8]

        x_res = sb(top, "x_res", [P, NT, D])
        xT_hi, xT_lo = split_sb(top, "xT", [P, KD, T])
        xn = sb(top, "xn", [P, TB, D])
        ident = sb(top, "ident", [P, P])
        rank = sb(top, "rank", [P, E])
        neg_half = sb(top, "neg_half", [P, TB])
        rw_raw = sb(top, "rw_raw", [P, KD, E])
        rw = sb(top, "rw", [P, KD, 2, E], F32R)
        NORMS = ("a", "b", "b2", "c", "y")
        stats = {n: sb(top, f"stats_{n}", [P, NT, 6]) for n in NORMS}
        mv = {n: sb(top, f"mv_{n}", [P, NT, 2]) for n in NORMS}
        var_eps = {n: sb(top, f"var_eps_{n}", [P, NT]) for n in NORMS}
        rstd = {n: sb(top, f"rstd_{n}", [P, NT]) for n in NORMS}
        shift = {n: sb(top, f"shift_{n}", [P, TB]) for n in ("b", "b2", "y")}
        logitT = sb(top, "logitT", [2 * E, T])
        logit2 = sb(top, "logit2", [P, NT, 2 * E])
        logit = sb(top, "logit", [P, NT, E])
        r_gap = sb(top, "r_gap", [P, 2, NT, E])
        r_exp = sb(top, "r_exp", [P, 2, NT, E])
        r_hot = sb(top, "r_hot", [P, 2, NT, E])
        r_keep = sb(top, "r_keep", [P, 2, NT, E])
        r_tmp = [sb(top, f"r_tmp{i}", [P, NT, E]) for i in range(5)]
        r_top = sb(top, "r_top", [P, 2, NT])
        r_red = sb(top, "r_red", [P, 2, NT])
        r_sum = sb(top, "r_sum", [P, 2, NT])
        r_mult = sb(top, "r_mult", [P, 2, NT])
        dense_w = sb(top, "dense_w", [P, NT, E])
        expert_w = sb(top, "expert_w", [P, NT])
        activated = sb(top, "activated", [P, 2, S])
        hid = sb(top, "hid", [P, 2, S])
        wo_raw = sb(top, "wo_raw", [P, KD, D])
        y_sb = wo_raw
        down_raw = wo_raw

        w1 = ExitStack()
        wkv_raw = sb(w1, "wkv_raw", [P, KD, 2 * DH])
        wq_hi, wq_lo = split_sb(w1, "wq", [P, KD, D])
        wkv_hi, wkv_lo = split_sb(w1, "wkv", [P, KD, 2 * DH])
        w1.close()
        gu_raw = sb(top, "gu_raw", [P, 2, 2, KD, P])
        guT_hi, guT_lo = split_sb(top, "guT", [P, 2, 2, KD, P])

        ab = ExitStack()
        w_raw = sb(ab, "w_raw", [P, KD, D])
        nw_row = sb(ab, "nw_row", [P, D])
        nb_row = sb(ab, "nb_row", [P, D])
        ow_row = sb(ab, "ow_row", [P, D])
        ob_row = sb(ab, "ob_row", [P, D])
        wo_hi, wo_lo = split_sb(ab, "wo", [P, KD, D])
        a_ = ExitStack()
        ctxT_raw = sb(a_, "ctxT_raw", [P, 2, KD, 2 * P])
        ctxN_raw = sb(a_, "ctxN_raw", [P, 2, 2, D])
        ctxT_hi, ctxT_lo = split_sb(a_, "ctxT", [P, 2, KD, P])
        ctxN_hi, ctxN_lo = split_sb(a_, "ctxN", [P, 2, D])
        hidT_hi, hidT_lo = split_sb(a_, "hidT", [P, 2, S])
        a_.close()
        b_ = ExitStack()
        probT_hi, probT_lo = split_sb(b_, "probT", [P, 2, KD, S])
        prob = sb(b_, "prob", [P, SLOTS, S])
        q_o = sb(b_, "q_o", [P, PAIRS, 2, S], F32R)
        kT_hi, kT_lo = split_sb(b_, "kT", [P, S])
        vT = activated[:, 0, :]
        vp_hi, vp_lo = split_sb(b_, "vp", [P, TB, 3, DH])
        neg_max = activated[:, 1, 0:B * UNITS]
        row_sum = sb(b_, "row_sum", [P, B * UNITS])
        row_inv = sb(b_, "row_inv", [P, B * UNITS])
        b_.close()
        ab.close()
        c_ = ExitStack()
        dnT_hi, dnT_lo = split_sb(c_, "dnT", [P, NF, D])
        hT_hi, hT_lo = split_sb(c_, "hT", [P, NF, T])
        c_.close()

        const_ready = sem("const_ready")
        x_loaded = [sem(f"x_loaded{t}") for t in range(TB)]
        x_rest_loaded = sem("x_rest_loaded")
        w_loaded, small_loaded = sem("w_loaded"), sem("small_loaded")
        norm_stat = {n: sem(f"norm_{n}_stat") for n in NORMS}
        norm_var = {n: sem(f"norm_{n}_var") for n in NORMS}
        norm_rstd = {n: sem(f"norm_{n}_rstd") for n in NORMS}
        norm_shift = {n: sem(f"norm_{n}_shift") for n in ("b", "b2", "y")}
        b_plain, b_scaled, b_weighted = sem("norm_b_plain"), sem("norm_b_scaled"), sem("norm_b_weighted")
        y_scaled, y_weighted, x_biased = sem("norm_y_scaled"), sem("norm_y_weighted"), sem("x_biased")
        xn_ready = {n: sem(f"xn_{n}_ready") for n in "abc"}
        xn_turned = {n: sem(f"xn_{n}_turned") for n in "abc"}
        xT_hi_done = {n: sem(f"xT_{n}_hi") for n in "abc"}
        xT_lo_done = {n: sem(f"xT_{n}_lo") for n in "abc"}
        ctxT_loaded = [sem("ctxT_loaded0"), sem("ctxT_loaded1")]
        ctxN_loaded = [sem("ctxN_loaded0"), sem("ctxN_loaded1")]
        ctxT_hi_done, ctxT_lo_done = sem("ctxT_hi_done"), sem("ctxT_lo_done")
        ctxN_hi_done, ctxN_lo_done = sem("ctxN_hi_done"), sem("ctxN_lo_done")
        x1_done, gelu_done, hid_done = sem("x1_done"), sem("gelu_done"), sem("hid_done")
        hidT_hi_done, hidT_lo_done = sem("hidT_hi_done"), sem("hidT_lo_done")
        cross_done, cross_added = sem("cross_done"), sem("cross_added")
        w_hi_done, w_lo_done, pads_zero = sem("w_hi_done"), sem("w_lo_done"), sem("pads_zero")
        proj_done, proj_hi_done, proj_lo_done = sem("proj_done"), sem("proj_hi_done"), sem("proj_lo_done")
        vT_done, v_turned, v_hi_done, v_lo_done = sem("vT_done"), sem("v_turned"), sem("v_hi_done"), sem("v_lo_done")
        sim_done, max_done, exp_done = sem("sim_done"), sem("max_done"), sem("exp_done")
        inv_done, prob_done = sem("inv_done"), sem("prob_done")
        prob_turned, probT_hi_done, probT_lo_done = sem("prob_turned"), sem("probT_hi_done"), sem("probT_lo_done")
        pv_done, oT_hi_done, oT_lo_done = sem("pv_done"), sem("oT_hi_done"), sem("oT_lo_done")
        y_begun, y_done, y_copied, self_added = sem("y_begun"), sem("y_done"), sem("y_copied"), sem("self_added")
        gu_loaded = [sem("gu_loaded0"), sem("gu_loaded1")]
        down_loaded = [sem("down_loaded0"), sem("down_loaded1")]
        rw_hi_done, rw_lo_done = sem("rw_hi_done"), sem("rw_lo_done")
        logits_done, logits_copied, logits_turned = sem("logits_done"), sem("logits_copied"), sem("logits_turned")
        route_step, route_gap, route_exp = sem("route_step"), sem("route_gap"), sem("route_exp")
        guT_hi_done, guT_lo_done = sem("guT_hi_done"), sem("guT_lo_done")
        dnT_hi_done, dnT_lo_done = sem("dnT_hi_done"), sem("dnT_lo_done")
        gate_done, up_done, silu_done, act_done = sem("gate_done"), sem("up_done"), sem("silu_done"), sem("act_done")
        hT_hi_done, hT_lo_done = sem("hT_hi_done"), sem("hT_lo_done")
        down_done, weight_picked, combined = sem("down_done"), sem("weight_picked"), sem("combined")
        stored = sem("stored")

        def f32(ap):
            return ap.bitcast(F32)

        def quarters(b):
            return b[:, :].rearrange("p (c q) -> p c q", c=4)

        def tile_cols(t):
            return slice(t * P, (t + 1) * P)

        USES = 1 + PAIRS
        LOS = 2 + 2 * PAIRS

        def split_to(p):
            return 2 + 2 * (p + 1)

        TURN_LAG, SPLIT_LAG = 5, 4
        OUT_LAG = SPLIT_LAG + TB + 2
        PIPE = UNITS + OUT_LAG

        def pair_out(u):
            w = u - OUT_LAG + 1
            return w // (2 * TB) if w >= 0 and w % (2 * TB) == 2 * TB - 1 else None

        ADD_AT, B_STAT_AT, B_SHIFT_AT, B2_STAT_AT, B2_SHIFT_AT = 0, 4, 11, 13, 19
        Y_SHIFT_AT, C_STAT_AT, C_NORM_AT = 3, 14, 33
        X_BIAS_AT = 20
        TURN_AT, TURN_EVERY = (26, 36), (3, 1)
        Q_AT = {1: 2, 2: 7, 3: 18}
        KV_AT = 37

        def tile_at(u, first, every):
            t = (u - first) // every
            return t if u >= first and (u - first) % every == 0 and t < TB else None

        ADD_ORDER = (2, 0, 1, 3)

        def q_at(u):
            return [p for p in Q_AT if Q_AT[p] == u]

        def group(n, g):
            if n == "a":
                return (range(0, TB // 2), range(TB // 2, TB), range(TB, NT))[g]
            return range(TB * g, TB * g + TB)

        def hidden_order(e_first):
            return [(c, s) for s in range(2) for c in range(NF)] if e_first else [(c, s) for c in range(NF) for s in range(2)]

        NORM_TURN, LOGITS_AT, ROUTE_AT = NF - 1, NF, NF + 2

        CTX_TURN = ({5: (TB, TB + 1), 6: (TB + 2, TB + 3)}, {8: (0, 1), 9: (2, 3)})

        def landed_at(g):
            return 16 * (g // 4 + 1)

        block = top.enter_context(nc.Block())

        @block.sync
        def _(sp):
            def load_ctx(j, s):
                sp.dma_start(ctxT_raw[:, s], ctxT_in[bass.ds(j, 1)].rearrange("a p c f -> p (a c) f")).then_inc(ctxT_loaded[s], 16)
                sp.dma_start(ctxN_raw[:, s], ctxN_pairs[bass.ds(j, 1)].rearrange("a p u d -> p (a u) d")).then_inc(ctxN_loaded[s], 16)

            for t in range(TB):
                sp.dma_start(x_res[:, t, :], x_dram[:, t, :]).then_inc(x_loaded[t], 16)
            load_ctx(0, 0)
            sp.dma_start(x_res[:, TB:NT, :], x_dram[:, TB:NT, :]).then_inc(x_rest_loaded, 16)
            load_ctx(1, 1)
            sp.dma_start(w_raw[:], Wq.rearrange("(c p) n -> p c n", p=P)).then_inc(w_loaded, 16)
            sp.dma_start(wo_raw[:], Wo.rearrange("(c p) n -> p c n", p=P)).then_inc(w_loaded, 16)
            sp.dma_start(wkv_raw[:], Wkv.rearrange("(c p) n -> p c n", p=P)).then_inc(w_loaded, 16)
            for row, w in ((nw_row, norm_w), (nb_row, norm_b), (ow_row, out_norm_w), (ob_row, out_norm_b)):
                sp.dma_start(row[:], w.rearrange("(a d) -> a d", a=1).broadcast_to([P, D])).then_inc(small_loaded, 16)
            sp.dma_start(rw_raw[:], routerT.rearrange("(c p) e -> p c e", p=P)).then_inc(small_loaded, 16)
            with sp.Fori(1, B * NC // 4) as i:
                for s in range(2):
                    sp.wait_ge(ctxT_lo_done, 4 * i + 2 * s - 2)
                    sp.wait_ge(ctxN_lo_done, 4 * i + 2 * s - 2)
                    load_ctx(2 * i + s, s)

            gate_upT_chunks = gate_upT.rearrange("e c p m j f -> (e c) p m j f")
            downT_pairs = downT.rearrange("e k p c d -> (e k) p c d")

            def load_gate_up(q, m, slot, first=False):
                if not first:
                    sp.wait_ge(guT_lo_done, m - 1)
                sp.dma_start(gu_raw[:, slot], gate_upT_chunks[bass.ds(q, 1)].rearrange("a p m j f -> p (a m) j f")).then_inc(gu_loaded[slot], 16)

            def load_down(e, k, first=False):
                if not first:
                    sp.wait_ge(dnT_lo_done, NF * e + 2 * k - 2)
                sp.dma_start(down_raw[:, 2 * (k % 2):2 * (k % 2) + 2, :],
                             downT_pairs[bass.ds(NF // 2 * e + k, 1)].rearrange("a p c d -> p (a c) d")).then_inc(down_loaded[k % 2], 16)

            sp.wait_ge(proj_done, USES * B)
            for m in range(NF):
                load_gate_up(m, m, m % 2, first=m < 2)
            sp.wait_ge(self_added, NT)
            for m in range(NF, 2 * NF):
                k = m - NF
                load_gate_up(k, m, m % 2)
                if k % 2 == 0:
                    load_down(0, k // 2, first=k < 4)
            with sp.Fori(1, E) as e:
                for c in range(NF):
                    load_gate_up(NF * e + c, NF * e + (NF + c), c % 2)
                    if c % 2 == 0:
                        load_down(e, c // 2)
            for t in range(NT):
                sp.wait_ge(combined, NT * (E - 1) + t + 1)
                sp.dma_start(out_dram[:, t, :], x_res[:, t, :]).then_inc(stored, 16)
            sp.wait_ge(stored, 16 * NT)

        @block.gpsimd
        def _(pool):
            nc.gpsimd.memset(ident[:], 0.0).then_inc(const_ready, 1)
            nc.gpsimd.memset(neg_half[:], -0.5).then_inc(const_ready, 1)
            for e in range(E):
                nc.gpsimd.memset(rank[:, e:e + 1], float(E - e)).then_inc(const_ready, 1)
            pool.wait_ge(const_ready, 2 + E)
            nc.gpsimd.affine_select(out=ident[:], in_=ident[:], compare_op=ALU.not_equal, fill=1.0,
                                    base=0, pattern=[[-1, P]], channel_multiplier=1).then_inc(const_ready, 1)

            def power(n, g):
                pool.wait_ge(norm_var[n], g + 1)
                tiles = slice(group(n, g).start, group(n, g).stop)
                nc.gpsimd.tensor_tensor(rstd[n][:, tiles], var_eps[n][:, tiles], neg_half[:, 0:len(group(n, g))],
                                        ALU.pow).then_inc(norm_rstd[n], 1)

            def ctx_lo(g, k):
                pool.wait_ge(ctxN_hi_done, g + 1)
                nc.gpsimd.tensor_tensor(ctxN_lo[:, k % 2, :], ctxN_raw[:, (k // 2) % 2, k % 2, :],
                                        f32(ctxN_hi[:, k % 2, :]), ALU.subtract).then_inc(ctxN_lo_done, 1)

            def weight_lo(k):
                pool.wait_ge(w_hi_done, k + 1)
                raw, hi, lo = ((w_raw, wq_hi, wq_lo), (wo_raw, wo_hi, wo_lo))[k // KD]
                c = k % KD
                nc.gpsimd.tensor_tensor(lo[:, c, :], raw[:, c, :], f32(hi[:, c, :]), ALU.subtract).then_inc(w_lo_done, 1)
                if k == 2 * KD - 1:
                    pool.wait_ge(w_hi_done, 2 * KD + 1)
                    nc.gpsimd.tensor_tensor(wkv_lo[:], wkv_raw[:], f32(wkv_hi[:]), ALU.subtract).then_inc(w_lo_done, 1)

            power("a", 0)
            power("a", 1)
            for g in range(4):
                ctx_lo(g, g)
            power("a", 2)
            with pool.Fori(1, NC // 4) as i:
                for k in range(4):
                    ctx_lo(4 * i + k, k)
            for k in range(9):
                ctx_lo(NC + k, k)
                if k == 2:
                    power("b", 0)
                if k == 4:
                    power("b2", 0)
                if k >= 1:
                    weight_lo(k - 1)

            def x_bias(t):
                pool.wait_ge(b_plain, t + 1)
                nc.gpsimd.tensor_tensor(x_res[:, t, :], x_res[:, t, :], ob_row[:], ALU.add).then_inc(x_biased, 1)

            pool.wait_ge(small_loaded, 16 * 5)
            for k in range(9, 12):
                ctx_lo(NC + k, k)
                x_bias(k - 9)
            x_bias(TB - 1)
            with pool.Fori(NC // 4 + 3, B * NC // 4) as i:
                for k in range(4):
                    ctx_lo(4 * i + k, k)

            for w in (vp_hi, vp_lo):
                for side in (0, 2):
                    nc.gpsimd.memset(f32(w[:, :, side, :]), 0.0).then_inc(pads_zero, 1)

            def b_weight(t):
                pool.wait_ge(b_scaled, TB + t + 1)
                nc.gpsimd.tensor_tensor(xn[:, t, :], xn[:, t, :], nw_row[:], ALU.mult).then_inc(b_weighted, 1)

            def b_bias(t):
                pool.wait_ge(b_weighted, t + 1)
                nc.gpsimd.tensor_tensor(xn[:, t, :], xn[:, t, :], nb_row[:], ALU.add).then_inc(xn_ready["b"], 1)

            def y_weight(t):
                pool.wait_ge(y_scaled, t + 1)
                nc.gpsimd.tensor_tensor(y_sb[:, t, :], y_sb[:, t, :], ow_row[:], ALU.mult).then_inc(y_weighted, 1)

            def y_add(t):
                pool.wait_ge(y_weighted, t + 1)
                pool.wait_ge(x_biased, t + 1)
                nc.gpsimd.tensor_tensor(x_res[:, t, :], x_res[:, t, :], y_sb[:, t, :], ALU.add).then_inc(self_added, 1)

            for b in range(B):
                for u in range(UNITS):
                    v = UNITS * b + u
                    pool.wait_ge(inv_done, v + 1)
                    p = prob[:, v % SLOTS, :]
                    nc.gpsimd.tensor_tensor(p, p, row_inv[:, v:v + 1].broadcast_to([P, S]), ALU.mult).then_inc(prob_done, 1)
                    for n, at in ((("b", B_STAT_AT + TB), ("b2", B2_STAT_AT + TB)),
                                  (("y", 0), ("c", C_STAT_AT + 3 * TB - 2)))[b]:
                        if u == at:
                            power(n, 1 - b)
                    t = tile_at(u, (B2_SHIFT_AT, Y_SHIFT_AT)[b] + 1, 3)
                    if t is not None:
                        (b_weight, y_weight)[b](t)
                    t = tile_at(u, (B2_SHIFT_AT, Y_SHIFT_AT)[b] + 2, 3)
                    if t is not None:
                        (b_bias, y_add)[b](t)
                    t = tile_at(u, X_BIAS_AT, 2)
                    if t is not None and b == 1:
                        x_bias(TB + t)
            power("y", 1)
            power("c", 1)

        @block.scalar
        def _(act):
            def xT_hi_tile(n, t, banks):
                act.wait_ge(xn_turned[n], t + 1)
                nc.scalar.activation(xT_hi[:, :, tile_cols(t)], quarters(banks[t % len(banks)]), ACT.Copy).then_inc(xT_hi_done[n], 1)

            for t in range(TB):
                xT_hi_tile("a", t, bank)

            def ctxT_hi_step(g, k, landed, first=False):
                act.wait_ge(ctxT_loaded[(k // 2) % 2], landed)
                if not first:
                    act.wait_ge(x1_done, g - 1)
                nc.scalar.activation(ctxT_hi[:, k % 2], ctxT_raw[:, (k // 2) % 2, :, tile_cols(k % 2)],
                                     ACT.Copy).then_inc(ctxT_hi_done, 1)

            def gelu_step(g, k, first=False):
                act.wait_ge(x1_done, g + 1)
                if not first:
                    act.wait_ge(hid_done, g - 1)
                nc.scalar.activation(activated[:, k % 2, :], X1[k % 2][:, :], ACT.Gelu_apprx_tanh).then_inc(gelu_done, 1)

            def hid_hi_step(g, k, first=False):
                act.wait_ge(hid_done, g + 1)
                if not first:
                    act.wait_ge(cross_done, g - 1)
                nc.scalar.activation(hidT_hi[:, k % 2, :], hid[:, k % 2, :], ACT.Copy).then_inc(hidT_hi_done, 1)

            def weight_hi(k):
                if k == 0:
                    act.wait_ge(w_loaded, 48)
                raw, hi = ((w_raw, wq_hi), (wo_raw, wo_hi))[k // KD]
                c = k % KD
                nc.scalar.activation(hi[:, c, :], raw[:, c, :], ACT.Copy).then_inc(w_hi_done, 1)
                if k == 2 * KD - 1:
                    nc.scalar.activation(wkv_hi[:], wkv_raw[:], ACT.Copy).then_inc(w_hi_done, 1)

            def cross_step(g, k, landed, ahead2=True, ahead1=True, first=False):
                if ahead2:
                    ctxT_hi_step(g + 2, k + 2, landed)
                if ahead1:
                    gelu_step(g + 1, k + 1, first)
                    hid_hi_step(g + 1, k + 1, first)

            for k in range(2):
                ctxT_hi_step(k, k, landed_at(k), first=True)
            gelu_step(0, 0, first=True)
            hid_hi_step(0, 0, first=True)
            for b in range(B):
                g0 = b * NC
                for k in range(HEAD_STEPS):
                    for t in CTX_TURN[b].get(k, ()):
                        xT_hi_tile("ab"[b], t, TURN)
                    cross_step(g0 + k, k, landed_at(g0 + k + 2), first=(b == 0 and k == 0))
                    if b == 1 and k < 2 * KD:
                        weight_hi(k)
                with act.Fori(HEAD_STEPS // 4, NC // 4 - 1) as i:
                    for k in range(4):
                        cross_step(4 * i + (g0 + k), k, 16 * i + landed_at(g0 + k + 2))
                for k in range(NC - 4, NC):
                    last = b == B - 1
                    cross_step(g0 + k, k, landed_at(g0 + k + 2), ahead2=not last or k < NC - 2, ahead1=not last or k < NC - 1)

            def guT_hi_step(m, slot, landed, free=None):
                act.wait_ge(gu_loaded[slot], landed)
                if free is not None:
                    act.wait_ge(up_done, free)
                nc.scalar.activation(guT_hi[:, slot], gu_raw[:, slot], ACT.Copy).then_inc(guT_hi_done, 1)

            def k_hi(b):
                act.wait_ge(proj_done, USES * b + 1)
                ps = K_BANK[b]
                nc.scalar.activation(vT[DH:P, :], ps[DH:P, :], ACT.Copy).then_inc(vT_done, 1)
                for half in (slice(0, DH), slice(DH, P)):
                    nc.scalar.activation(kT_hi[half, :], ps[0:DH, :], ACT.Copy).then_inc(proj_hi_done, 1)

            def v_hi(b):
                act.wait_ge(v_turned, b + 1)
                if b == 1:
                    act.wait_ge(pv_done, HEADS)
                nc.scalar.activation(vp_hi[:, :, 1, :], V_BANK[b][:, 0:TB * DH].rearrange("p (t d) -> p t d", t=TB),
                                     ACT.Copy).then_inc(v_hi_done, 1)

            def q_hi(b, p, halves=(0, 1)):
                act.wait_ge(proj_done, USES * b + 2 + p)
                if b == 1:
                    if p < PAIRS - 1:
                        act.wait_ge(y_begun, 1)
                    else:
                        act.wait_ge(y_done, TB)
                for r in halves:
                    own = slice(r * DH, (r + 1) * DH)
                    nc.scalar.activation(q_o[own, p, r, :], Q_BANK[b][p][own, :], ACT.Copy,
                                         scale=SCALE).then_inc(proj_hi_done, 1)

            def y_copy(b):
                for t in range(TB):
                    act.wait_ge(y_done, TB * b + t + 1)
                    if b == 1:
                        act.wait_ge(self_added, t + 1)
                    nc.scalar.activation(y_sb[:, t, :], Y_OF[b][t][:, :], ACT.Copy).then_inc(y_copied, 1)

            def normalised(n, i, tile, src, done):
                act.wait_ge(norm_shift[n], 1)
                nc.scalar.activation(tile, src, ACT.Identity, bias=shift[n][:, i % TB:i % TB + 1],
                                     scale=rstd[n][:, i:i + 1]).then_inc(done, 1)

            k_hi(0)
            q_hi(0, 0)
            v_hi(0)
            for b in range(B):
                if b == 1:
                    q_hi(1, 0)
                    y_copy(0)

                for u in range(PIPE):
                    v = UNITS * b + u
                    if 0 <= u - SPLIT_LAG < UNITS:
                        w, i, h = v - SPLIT_LAG, (u - SPLIT_LAG) % TB, (u - SPLIT_LAG) // TB
                        act.wait_ge(prob_turned, w + 1)
                        if HEADS * b + h >= 2:
                            act.wait_ge(pv_done, HEADS * b + h - 1)
                        nc.scalar.activation(probT_hi[:, h % 2, :, tile_cols(i)], quarters(TURN[w % 2]),
                                             ACT.Copy).then_inc(probT_hi_done, 1)
                    if u < UNITS:
                        act.wait_ge(max_done, v + 1)
                        if v >= SLOTS:
                            act.wait_ge(prob_turned, v - SLOTS + 1)
                        nc.scalar.activation(prob[:, v % SLOTS, :], SIM[u % 3][:, :], ACT.Exp,
                                             bias=neg_max[:, v:v + 1], accum_out=row_sum[:, v:v + 1]).then_inc(exp_done, 1)
                    t = tile_at(u, B_SHIFT_AT + 1, 1)
                    if t is not None and b == 0:
                        if t == 0:
                            act.wait_ge(xn_turned["b"], TB)
                        normalised("b", TB + t, xn[:, t, :], x_res[:, TB + t, :], b_plain)
                    t = tile_at(u, (B2_SHIFT_AT, Y_SHIFT_AT)[b] + 1, 1)
                    if t is not None and b == 0:
                        normalised("b2", TB + t, xn[:, t, :], xn[:, t, :], b_scaled)
                    elif t is not None:
                        normalised("y", t, y_sb[:, t, :], y_sb[:, t, :], y_scaled)
                    for r in range(2):
                        for p in q_at(u - r):
                            q_hi(b, p, (r,))
                    t = tile_at(u, TURN_AT[b], TURN_EVERY[b])
                    if t is not None:
                        xT_hi_tile("bc"[b], (TB, 0)[b] + t, NORM_BANKS[b])
                    p = pair_out(u)
                    if p is not None:
                        act.wait_ge(pv_done, HEADS * b + 2 * p + 2)
                        nc.scalar.activation(q_o[:, p, 0, :], HEAD_OUT[p % 2][:, :], ACT.Copy).then_inc(oT_hi_done, 1)
                    if b == 0 and u == KV_AT:
                        k_hi(1)
                    if b == 0 and u == PIPE - 1:
                        v_hi(1)
                    if b == 1 and u == UNITS + TB:
                        nc.scalar.activation(rw[:, :, 0, :], rw_raw[:], ACT.Copy).then_inc(rw_hi_done, 1)

            def dnT_hi_step(e, c, landed, first):
                act.wait_ge(down_loaded[(c // 2) % 2], landed)
                if not first:
                    act.wait_ge(down_done, NT * e)
                nc.scalar.activation(dnT_hi[:, c, :], down_raw[:, c % 4, :], ACT.Copy).then_inc(dnT_hi_done, 1)

            def silu_step(n, v, first):
                act.wait_ge(gate_done, v + 1)
                if not first:
                    act.wait_ge(act_done, v - 1)
                nc.scalar.activation(activated[:, n % 2, :], GATE[n % 2][:, :], ACT.Silu).then_inc(silu_done, 1)

            def hT_hi_step(c, s, n, v):
                act.wait_ge(act_done, v + 1)
                nc.scalar.activation(hT_hi[:, c, s * S:(s + 1) * S], hid[:, n % 2, :], ACT.Copy).then_inc(hT_hi_done, 1)

            def expert(e, first, last):
                for n, (c, s) in enumerate(hidden_order(first)):
                    v = 2 * NF * e + n
                    k = n - NF + 1 if first else n // 2
                    if first and n == NORM_TURN:
                        for t in range(TB, NT):
                            xT_hi_tile("c", t, Y_OF[1])
                    if first:
                        guT_hi_step(n + 2, n % 2, 16 * (n // 2 + 2), n + 1)
                    if 0 <= k < NF and (first or n % 2 == 0):
                        dnT_hi_step(e, k, 32 * e + 16 * (k // 4 + 1), first)
                    silu_step(n, v, first and n < 2)
                    hT_hi_step(c, s, n, v)
                    if not first and n % 2 == 1 and not (last and k + 2 >= NF):
                        guT_hi_step(NF * e + NF + k + 2, k % 2, 64 * e + 16 * (NF // 2 + k // 2 + 2), v + 1)
                    if first and n == ROUTE_AT + 3:
                        act.wait_ge(route_gap, 1)
                        nc.scalar.activation(r_exp[:], r_gap[:], ACT.Exp, scale=-1.0).then_inc(route_exp, 1)

            for m in range(2):
                guT_hi_step(m, m, 16)
            y_copy(1)
            expert(0, True, False)
            with act.Fori(1, E - 1) as e:
                expert(e, False, False)
            expert(E - 1, False, True)

        @block.vector
        def _(dve):
            V = nc.vector

            def stat_tile(n, src, t):
                V.bn_stats(stats[n][:, t, :], src).then_inc(norm_stat[n], 1)

            def stat_end(n, g):
                tiles = group(n, g)
                dve.wait_ge(norm_stat[n], tiles.start + tiles.stop)
                for t in tiles:
                    V.bn_aggr(mv[n][:, t, :], stats[n][:, t, :]).then_inc(norm_stat[n], 1)
                dve.wait_ge(norm_stat[n], 2 * tiles.stop)
                tiles = slice(tiles.start, tiles.stop)
                V.tensor_scalar_add(var_eps[n][:, tiles], mv[n][:, tiles, 1], EPS).then_inc(norm_var[n], 1)

            def shift_tiles(n, g):
                dve.wait_ge(norm_rstd[n], g + 1)
                tiles = slice(group(n, g).start, group(n, g).stop)
                V.scalar_tensor_tensor(shift[n][:], mv[n][:, tiles, 0], -1.0, rstd[n][:, tiles],
                                       ALU.mult, ALU.mult).then_inc(norm_shift[n], 1)

            def norm_tile(n, t, done):
                V.tensor_scalar(xn[:, t % TB, :], x_res[:, t, :], mv[n][:, t, 0:1], rstd[n][:, t:t + 1],
                                ALU.subtract, ALU.mult).then_inc(done, 1)

            def xT_lo_tile(n, t, banks):
                dve.wait_ge(xT_hi_done[n], t + 1)
                V.tensor_tensor(xT_lo[:, :, tile_cols(t)], quarters(banks[t % len(banks)]), f32(xT_hi[:, :, tile_cols(t)]),
                                ALU.subtract).then_inc(xT_lo_done[n], 1)

            def b_first(b, t):
                norm_tile("b", TB * b + t, b_plain)

            def b_second_stat(b, t):
                dve.wait_ge(b_plain, TB * b + t + 1)
                stat_tile("b2", xn[:, t, :], TB * b + t)

            def b_scale(t):
                V.scalar_tensor_tensor(xn[:, t, :], xn[:, t, :], mv["b2"][:, t, 0:1], nw_row[:],
                                       ALU.subtract, ALU.mult).then_inc(b_scaled, 1)

            def b_last(t):
                dve.wait_ge(b_scaled, t + 1)
                V.scalar_tensor_tensor(xn[:, t, :], xn[:, t, :], rstd["b2"][:, t:t + 1], nb_row[:],
                                       ALU.mult, ALU.add).then_inc(xn_ready["b"], 1)

            for g in range(2):
                for t in group("a", g):
                    dve.wait_ge(x_loaded[t], 16)
                    stat_tile("a", x_res[:, t, :], t)
                stat_end("a", g)
            for g in range(2):
                dve.wait_ge(norm_rstd["a"], g + 1)
                for t in group("a", g):
                    norm_tile("a", t, xn_ready["a"])
            for t in range(TB):
                xT_lo_tile("a", t, bank)

            def ctxT_lo_step(g, k):
                dve.wait_ge(ctxT_hi_done, g + 1)
                V.tensor_tensor(ctxT_lo[:, k % 2], ctxT_raw[:, (k // 2) % 2, :, tile_cols(k % 2)], f32(ctxT_hi[:, k % 2]),
                                ALU.subtract).then_inc(ctxT_lo_done, 1)

            def ctxN_hi_step(g, k, landed, first=False):
                dve.wait_ge(ctxN_loaded[(k // 2) % 2], landed)
                if not first:
                    dve.wait_ge(cross_done, g - 1)
                V.tensor_copy(ctxN_hi[:, k % 2, :], ctxN_raw[:, (k // 2) % 2, k % 2, :]).then_inc(ctxN_hi_done, 1)

            def hid_step(g, k, first=False):
                dve.wait_ge(gelu_done, g + 1)
                if not first:
                    dve.wait_ge(hidT_lo_done, g - 1)
                V.tensor_tensor(hid[:, k % 2, :], X1[k % 2][:, :], activated[:, k % 2, :], ALU.mult).then_inc(hid_done, 1)

            def hid_lo_step(g, k):
                dve.wait_ge(hidT_hi_done, g + 1)
                V.tensor_tensor(hidT_lo[:, k % 2, :], hid[:, k % 2, :], f32(hidT_hi[:, k % 2, :]),
                                ALU.subtract).then_inc(hidT_lo_done, 1)

            def a_norm_part(k):
                if k in (1, 2):
                    if k == 1:
                        dve.wait_ge(x_rest_loaded, 16)
                    for t in range(TB + TB // 2 * (k - 1), TB + TB // 2 * k):
                        stat_tile("a", x_res[:, t, :], t)
                    if k == 2:
                        stat_end("a", 2)
                elif k == 3:
                    dve.wait_ge(norm_rstd["a"], 3)
                    dve.wait_ge(xn_turned["a"], TB)
                    for t in range(TB, NT):
                        norm_tile("a", t, xn_ready["a"])

            def b_norm_part(k):
                tiles = range(TB)
                if k == 1:
                    for t in tiles:
                        dve.wait_ge(cross_added, t + 1)
                        stat_tile("b", x_res[:, t, :], t)
                    stat_end("b", 0)
                elif k == 2:
                    dve.wait_ge(norm_rstd["b"], 1)
                    for t in tiles:
                        b_first(0, t)
                elif k == 3:
                    for t in tiles:
                        b_second_stat(0, t)
                    stat_end("b2", 0)
                elif k == 4:
                    dve.wait_ge(small_loaded, 16 * 5)
                    for t in tiles:
                        b_scale(t)
                elif k == 5:
                    dve.wait_ge(norm_rstd["b2"], 1)
                    for t in tiles:
                        b_last(t)

            def cross_step(g, k, landed, ahead2=True, ahead1=True, first=False):
                if ahead2:
                    ctxT_lo_step(g + 2, k + 2)
                if ahead1:
                    ctxN_hi_step(g + 1, k + 1, landed, first)
                    hid_step(g + 1, k + 1, first)
                    hid_lo_step(g + 1, k + 1)

            for k in range(2):
                ctxT_lo_step(k, k)
            ctxN_hi_step(0, 0, landed_at(0), first=True)
            hid_step(0, 0, first=True)
            hid_lo_step(0, 0)
            for b in range(B):
                g0 = b * NC
                if b == 1:
                    dve.wait_ge(cross_done, NC)
                    for t in range(TB):
                        xt = x_res[:, t, :]
                        V.tensor_tensor(xt, ACC[t][:, :], xt, ALU.add).then_inc(cross_added, 1)
                for k in range(HEAD_STEPS):
                    for t in CTX_TURN[b].get(k, ()):
                        xT_lo_tile("ab"[b], t, TURN)
                    cross_step(g0 + k, k, landed_at(g0 + k + 1), first=(b == 0 and k == 0))
                    (a_norm_part, b_norm_part)[b](k)
                with dve.Fori(HEAD_STEPS // 4, NC // 4 - 1) as i:
                    for k in range(4):
                        cross_step(4 * i + (g0 + k), k, 16 * i + landed_at(g0 + k + 1))
                for k in range(NC - 4, NC):
                    last = b == B - 1
                    cross_step(g0 + k, k, landed_at(g0 + k + 1), ahead2=not last or k < NC - 2, ahead1=not last or k < NC - 1)

            def guT_lo_step(m, slot):
                dve.wait_ge(guT_hi_done, m + 1)
                V.tensor_tensor(guT_lo[:, slot], gu_raw[:, slot], f32(guT_hi[:, slot]), ALU.subtract).then_inc(guT_lo_done, 1)

            def k_lo(b):
                dve.wait_ge(proj_hi_done, LOS * b + 2)
                for half in (slice(0, DH), slice(DH, P)):
                    V.tensor_tensor(kT_lo[half, :], K_BANK[b][0:DH, :], f32(kT_hi[0:DH, :]), ALU.subtract).then_inc(proj_lo_done, 1)

            def v_lo(b):
                dve.wait_ge(v_hi_done, b + 1)
                V.tensor_tensor(vp_lo[:, :, 1, :], V_BANK[b][:, 0:TB * DH].rearrange("p (t d) -> p t d", t=TB),
                                f32(vp_hi[:, :, 1, :]), ALU.subtract).then_inc(v_lo_done, 1)

            def q_lo(b, p, halves=(0, 1)):
                for r in halves:
                    dve.wait_ge(proj_hi_done, LOS * b + split_to(p) - 1 + r)
                    own, other = slice(r * DH, (r + 1) * DH), slice((1 - r) * DH, (2 - r) * DH)
                    V.scalar_tensor_tensor(q_o[other, p, r, :], Q_BANK[b][p][own, :], SCALE, f32(q_o[own, p, r, :]),
                                           ALU.mult, ALU.subtract).then_inc(proj_lo_done, 1)

            k_lo(0)
            q_lo(0, 0)
            v_lo(0)

            def b_behind(u):
                t = tile_at(u, ADD_AT, 1)
                if t is not None:
                    if t == 0:
                        dve.wait_ge(cross_done, B * NC)
                    xt = x_res[:, TB + ADD_ORDER[t], :]
                    V.tensor_tensor(xt, ACC[ADD_ORDER[t]][:, :], xt, ALU.add).then_inc(cross_added, 1)
                t = tile_at(u, B_STAT_AT, 1)
                if t is not None:
                    dve.wait_ge(cross_added, TB + t + 1)
                    stat_tile("b", x_res[:, TB + ADD_ORDER[t], :], TB + ADD_ORDER[t])
                if u == B_STAT_AT + TB:
                    stat_end("b", 1)
                if u == B_SHIFT_AT:
                    shift_tiles("b", 1)
                t = tile_at(u, B2_STAT_AT, 1)
                if t is not None:
                    b_second_stat(1, t)
                if u == B2_STAT_AT + TB:
                    stat_end("b2", 1)
                if u == B2_SHIFT_AT:
                    shift_tiles("b2", 1)

            def c_behind(u):
                if u == Y_SHIFT_AT:
                    shift_tiles("y", 0)
                t = tile_at(u, C_STAT_AT, 3)
                if t is not None:
                    dve.wait_ge(self_added, t + 1)
                    stat_tile("c", x_res[:, t, :], t)
                if u == C_STAT_AT + 3 * TB - 2:
                    stat_end("c", 0)
                t = tile_at(u, C_NORM_AT, 1)
                if t is not None:
                    if t == 0:
                        dve.wait_ge(norm_rstd["c"], 1)
                        dve.wait_ge(xn_turned["b"], NT)
                    norm_tile("c", t, xn_ready["c"])

            for b in range(B):
                if b == 1:
                    q_lo(1, 0)
                    for t in range(TB):
                        dve.wait_ge(y_copied, t + 1)
                        stat_tile("y", y_sb[:, t, :], t)
                    stat_end("y", 0)

                for u in range(PIPE):
                    v = UNITS * b + u
                    if u < UNITS:
                        dve.wait_ge(sim_done, v + 1)
                        V.tensor_reduce(neg_max[:, v:v + 1], SIM[u % 3][:, :], AX_X, ALU.max, negate=True).then_inc(max_done, 1)
                    if 0 <= u - 1 < UNITS:
                        dve.wait_ge(exp_done, v)
                        V.reciprocal(row_inv[:, v - 1:v], row_sum[:, v - 1:v]).then_inc(inv_done, 1)
                    if 0 <= u - SPLIT_LAG < UNITS:
                        w, i, h = v - SPLIT_LAG, (u - SPLIT_LAG) % TB, (u - SPLIT_LAG) // TB
                        dve.wait_ge(probT_hi_done, w + 1)
                        V.tensor_tensor(probT_lo[:, h % 2, :, tile_cols(i)], quarters(TURN[w % 2]),
                                        f32(probT_hi[:, h % 2, :, tile_cols(i)]), ALU.subtract).then_inc(probT_lo_done, 1)
                    (b_behind, c_behind)[b](u)
                    for r in range(2):
                        for p in q_at(u - 1 - r):
                            q_lo(b, p, (r,))
                    t = tile_at(u, TURN_AT[b] + 1, TURN_EVERY[b])
                    if t is not None:
                        xT_lo_tile("bc"[b], (TB, 0)[b] + t, NORM_BANKS[b])
                    p = pair_out(u - 1)
                    if p is not None:
                        dve.wait_ge(oT_hi_done, PAIRS * b + p + 1)
                        V.tensor_tensor(q_o[:, p, 1, :], HEAD_OUT[p % 2][:, :], f32(q_o[:, p, 0, :]),
                                        ALU.subtract).then_inc(oT_lo_done, 1)
                    if b == 0 and u == KV_AT:
                        k_lo(1)
                    if b == 1 and u == UNITS + TB:
                        dve.wait_ge(rw_hi_done, 1)
                        V.tensor_tensor(rw[:, :, 1, :], rw_raw[:], f32(rw[:, :, 0, :]), ALU.subtract).then_inc(rw_lo_done, 1)
                if b == 0:
                    v_lo(1)

            def over_experts(ap):
                return ap.unsqueeze(2).broadcast_to([P, NT, E])

            def route_parts():
                step = [0]

                def then(ins):
                    step[0] += 1
                    ins.then_inc(route_step, 1)
                    dve.wait_ge(route_step, step[0])

                first, second = 0, 1
                magnitude, limit, cand, others, rest = r_tmp
                ranks = rank[:].unsqueeze(1).broadcast_to([P, NT, E])
                dve.wait_ge(logits_turned, 1)
                then(V.tensor_copy(logit2[:], TURN[0][:, 0:NT * 2 * E].rearrange("p (t e) -> p t e", e=2 * E)))
                then(V.tensor_tensor(logit[:], logit2[:, :, 0:E], logit2[:, :, E:], ALU.add))
                then(V.scalar_tensor_tensor(magnitude[:], logit[:], -1.0, logit[:], ALU.mult, ALU.max))
                for n, score in ((first, logit), (second, rest)):
                    top_b = over_experts(r_top[:, n, :])
                    then(V.tensor_reduce(r_top[:, n, :], score[:], AX_X, ALU.max))
                    then(V.tensor_tensor(cand[:], score[:], top_b, ALU.is_ge))
                    then(V.tensor_tensor(cand[:], cand[:], ranks, ALU.mult))
                    then(V.tensor_reduce(r_red[:, n, :], cand[:], AX_X, ALU.max))
                    then(V.tensor_tensor(r_hot[:, n], cand[:], over_experts(r_red[:, n, :]), ALU.is_equal))
                    yield
                    then(V.tensor_tensor(r_gap[:, n], top_b, logit[:], ALU.subtract))
                    then(V.tensor_tensor(limit[:], magnitude[:], top_b, ALU.max))
                    then(V.scalar_tensor_tensor(r_keep[:, n], limit[:], JITTER, r_gap[:, n], ALU.mult, ALU.is_ge))
                    if n == first:
                        then(V.tensor_scalar(others[:], r_hot[:, n], -1.0, 1.0, ALU.mult, ALU.add))
                        then(V.tensor_tensor(rest[:], logit[:], others[:], ALU.mult))
                        then(V.scalar_tensor_tensor(rest[:], r_hot[:, n], LOWEST, rest[:], ALU.mult, ALU.add))
                        yield
                then(V.tensor_tensor(r_keep[:, second], r_keep[:, second], others[:], ALU.mult))
                V.tensor_scalar_max(r_gap[:, second], r_gap[:, second], 0.0).then_inc(route_gap, 1)
                yield
                dve.wait_ge(route_exp, 1)
                then(V.tensor_tensor(r_keep[:], r_keep[:], r_exp[:], ALU.mult))
                then(V.tensor_reduce(r_sum[:], r_keep[:], AX_X, ALU.add))
                then(V.reciprocal(r_mult[:], r_sum[:]))
                for n in (first, second):
                    then(V.tensor_tensor(r_hot[:, n], r_hot[:, n], over_experts(r_mult[:, n, :]), ALU.mult))
                then(V.tensor_tensor(dense_w[:], r_hot[:, first], r_hot[:, second], ALU.add))
                yield

            route = route_parts()

            def hidden_step(c, s, n, v, first):
                dve.wait_ge(silu_done, v + 1)
                dve.wait_ge(up_done, v + 1)
                if not first:
                    dve.wait_ge(hT_lo_done, v - 1)
                V.tensor_tensor(hid[:, n % 2, :], UP[n % 2][:, :], activated[:, n % 2, :], ALU.mult).then_inc(act_done, 1)
                dve.wait_ge(hT_hi_done, v + 1)
                V.tensor_tensor(hT_lo[:, c, s * S:(s + 1) * S], hid[:, n % 2, :],
                                f32(hT_hi[:, c, s * S:(s + 1) * S]), ALU.subtract).then_inc(hT_lo_done, 1)

            def last_norm_part(n):
                tiles = range(TB, NT)
                if n == 0:
                    for t in tiles:
                        dve.wait_ge(y_copied, t + 1)
                        stat_tile("y", y_sb[:, t % TB, :], t)
                    stat_end("y", 1)
                elif n == 1:
                    for t in tiles:
                        V.scalar_tensor_tensor(y_sb[:, t % TB, :], y_sb[:, t % TB, :], mv["y"][:, t, 0:1], ow_row[:],
                                               ALU.subtract, ALU.mult).then_inc(y_scaled, 1)
                elif n == 2:
                    dve.wait_ge(norm_rstd["y"], 2)
                    for t in tiles:
                        dve.wait_ge(y_scaled, t + 1)
                        dve.wait_ge(x_biased, t + 1)
                        V.scalar_tensor_tensor(x_res[:, t, :], y_sb[:, t % TB, :], rstd["y"][:, t:t + 1], x_res[:, t, :],
                                               ALU.mult, ALU.add).then_inc(self_added, 1)
                elif n == 3:
                    for t in tiles:
                        dve.wait_ge(self_added, t + 1)
                        stat_tile("c", x_res[:, t, :], t)
                    stat_end("c", 1)
                elif n == 4:
                    dve.wait_ge(norm_rstd["c"], 2)
                    dve.wait_ge(xn_turned["c"], TB)
                    for t in tiles:
                        norm_tile("c", t, xn_ready["c"])

            def expert(e, first, last):
                for n, (c, s) in enumerate(hidden_order(first)):
                    v = 2 * NF * e + n
                    k = n - NF + 1 if first else n // 2
                    if first and n == NORM_TURN:
                        for t in range(TB, NT):
                            xT_lo_tile("c", t, Y_OF[1])
                    if first and n == LOGITS_AT:
                        for half in range(2):
                            dve.wait_ge(logits_done, half + 1)
                            V.tensor_copy(logitT[:, half * S:(half + 1) * S], TURN[half][0:2 * E, :]).then_inc(logits_copied, 1)
                    if first:
                        guT_lo_step(n + 2, n % 2)
                    if 0 <= k < NF and (first or n % 2 == 0):
                        dve.wait_ge(dnT_hi_done, NF * e + k + 1)
                        V.tensor_tensor(dnT_lo[:, k, :], down_raw[:, k % 4, :], f32(dnT_hi[:, k, :]),
                                        ALU.subtract).then_inc(dnT_lo_done, 1)
                    hidden_step(c, s, n, v, first and n < 2)
                    if first:
                        last_norm_part(n)
                        if ROUTE_AT <= n < ROUTE_AT + 5:
                            next(route)
                    elif n % 2 == 1 and not (last and k + 2 >= NF):
                        guT_lo_step(NF * e + (NF + k + 2), k % 2)
                if not first:
                    dve.wait_ge(combined, NT * e)
                V.tensor_copy(expert_w[:].unsqueeze(2), dense_w[:, :, bass.ds(e, 1)]).then_inc(weight_picked, 1)
                dve.wait_ge(weight_picked, e + 1)
                for t in range(NT):
                    dve.wait_ge(down_done, NT * e + (t + 1))
                    xt = x_res[:, t, :]
                    V.scalar_tensor_tensor(xt, DOWN_OUT[t % 2][:, :], expert_w[:, t:t + 1], xt,
                                           ALU.mult, ALU.add).then_inc(combined, 1)

            for m in range(2):
                guT_lo_step(m, m)
            expert(0, True, False)
            with dve.Fori(1, E - 1) as e:
                expert(e, False, False)
            expert(E - 1, False, True)

        @block.tensor
        def _(pe):
            def product(out_ap, pairs, start=True, stop=True):
                n = len(pairs)
                for i, ((l_hi, l_lo), (r_hi, r_lo)) in enumerate(pairs):
                    nc.tensor.matmul(out_ap, l_lo, r_hi, start=start and i == 0, stop=False)
                    nc.tensor.matmul(out_ap, l_hi, r_lo, start=False, stop=False)
                    last = nc.tensor.matmul(out_ap, l_hi, r_hi, start=False, stop=stop and i == n - 1)
                return last

            def turn(dst, src):
                for i in range(4):
                    last = nc.tensor.transpose(dst[:, tile_cols(i)], src[:, tile_cols(i)], ident[:])
                return last

            def xn_turn(n, t, banks):
                pe.wait_ge(xn_ready[n], t + 1)
                if t >= len(banks):
                    pe.wait_ge(xT_lo_done[n], t - len(banks) + 1)
                turn(banks[t % len(banks)], xn[:, t % TB, :]).then_inc(xn_turned[n], 1)

            def xT_cols(c, lo, n):
                return xT_hi[:, c, lo:lo + n], xT_lo[:, c, lo:lo + n]

            pe.wait_ge(const_ready, 3 + E)
            for t in range(TB):
                xn_turn("a", t, bank)
            pe.wait_ge(xT_lo_done["a"], TB)

            def x1_step(b, g, k, first=False):
                pe.wait_ge(ctxT_lo_done, g + 1)
                if not first:
                    pe.wait_ge(hid_done, g - 1)
                product(X1[k % 2][:, :],
                        [((ctxT_hi[:, k % 2, c, :], ctxT_lo[:, k % 2, c, :]), xT_cols(c, b * S, S))
                         for c in range(KD)]).then_inc(x1_done, 1)

            def cross_out(g, k, start, stop):
                pe.wait_ge(hidT_lo_done, g + 1)
                pe.wait_ge(ctxN_lo_done, g + 1)
                for t in range(TB):
                    last = product(ACC[t][:, :],
                                   [((hidT_hi[:, k % 2, tile_cols(t)], hidT_lo[:, k % 2, tile_cols(t)]),
                                     (ctxN_hi[:, k % 2, :], ctxN_lo[:, k % 2, :]))], start=start, stop=stop)
                last.then_inc(cross_done, 1)

            def k_and_v(b):
                pe.wait_ge(xT_lo_done["b"], TB * (b + 1))
                product(K_BANK[b][:, :], [((wkv_hi[:, c, :], wkv_lo[:, c, :]), xT_cols(c, b * S, S))
                                              for c in range(KD)]).then_inc(proj_done, 1)

            def v_turn(b):
                pe.wait_ge(vT_done, b + 1)
                for t in range(TB):
                    last = nc.tensor.transpose(V_BANK[b][:, t * DH:(t + 1) * DH], vT[DH:P, tile_cols(t)], ident[DH:P, DH:P])
                last.then_inc(v_turned, 1)

            def q_pair(b, p):
                if b == 0 and p == 0:
                    pe.wait_ge(hid_done, B * NC - 1)
                elif b == 0:
                    pe.wait_ge(cross_added, TB + 1 + p)
                elif p == 0:
                    pe.wait_ge(proj_lo_done, LOS + split_to(-1))
                elif p == PAIRS - 1:
                    pe.wait_ge(proj_lo_done, LOS + split_to(0))
                product(Q_BANK[b][p][:, :], [((wq_hi[:, c, tile_cols(p)], wq_lo[:, c, tile_cols(p)]), xT_cols(c, b * S, S))
                                                  for c in range(KD)]).then_inc(proj_done, 1)

            def cross_step(b, g, k, ahead1=True, start=False, stop=False, first=False):
                if ahead1:
                    x1_step(b, g + 1, k + 1, first)
                if b == 1 and start:
                    pe.wait_ge(cross_added, TB)
                cross_out(g, k, start, stop)

            x1_step(0, 0, 0, first=True)
            for b in range(B):
                g0 = b * NC
                for k in range(HEAD_STEPS):
                    for t in CTX_TURN[b].get(k, ()):
                        xn_turn("ab"[b], t, TURN)
                    cross_step(b, g0 + k, k, start=(k == 0), first=(b == 0 and k == 0))
                with pe.Fori(HEAD_STEPS // 4, NC // 4 - 1) as i:
                    for k in range(4):
                        cross_step(b, 4 * i + (g0 + k), k)
                for k in range(NC - 4, NC - 1):
                    cross_step(b, g0 + k, k)
                if b == 0:
                    pe.wait_ge(xT_lo_done["a"], NT)
                    cross_step(1, g0 + NC - 1, NC - 1, stop=True)
                else:
                    pe.wait_ge(w_lo_done, 2 * KD + 1)
                    k_and_v(0)
                    q_pair(0, 0)
                    cross_step(b, g0 + NC - 1, NC - 1, ahead1=False, stop=True)
                    v_turn(0)

            def y_begin(b):
                pe.wait_ge(oT_lo_done, PAIRS * (b + 1) - 1)
                for t in range(TB):
                    last = product(Y_OF[b][t][:, :],
                                   [((q_o[:, p, 0, tile_cols(t)], q_o[:, p, 1, tile_cols(t)]), (wo_hi[:, p, :], wo_lo[:, p, :]))
                                    for p in range(PAIRS - 1)], stop=False)
                last.then_inc(y_begun, 1)

            def y_end(b):
                pe.wait_ge(oT_lo_done, PAIRS * (b + 1))
                p = PAIRS - 1
                for t in range(TB):
                    product(Y_OF[b][t][:, :],
                            [((q_o[:, p, 0, tile_cols(t)], q_o[:, p, 1, tile_cols(t)]), (wo_hi[:, p, :], wo_lo[:, p, :]))],
                            start=False).then_inc(y_done, 1)

            pe.wait_ge(pads_zero, 4)
            for b in range(B):
                for u in range(PIPE):
                    v = UNITS * b + u
                    if u < UNITS:
                        h, i = u // TB, u % TB
                        if u % (2 * TB) == 0:
                            pe.wait_ge(proj_lo_done, LOS * b + split_to(h // 2))
                        if b == 1 and u < 3:
                            pe.wait_ge(y_copied, (1, 2, TB)[u])
                        if u == 2:
                            pe.wait_ge(cross_added, TB + 1)
                            pe.wait_ge(v_lo_done, b + 1)
                        if u >= 3:
                            pe.wait_ge(exp_done, v - 2)
                        q = q_o[:, h // 2, h % 2, tile_cols(i)]
                        nc.tensor.matmul(SIM[u % 3][:, :], q, kT_lo[:], start=True, stop=False)
                        nc.tensor.matmul(SIM[u % 3][:, :], q, kT_hi[:], start=False, stop=True).then_inc(sim_done, 1)
                    if u >= OUT_LAG:
                        h, j = (u - OUT_LAG) // TB, (u - OUT_LAG) % TB
                        if j == 0:
                            pe.wait_ge(probT_lo_done, TB * (HEADS * b + h + 1))
                            n = PAIRS * b + h // 2
                            if h % 2 == 0 and n >= 2:
                                pe.wait_ge(oT_lo_done, n - 1)
                            if b == 0 and h == HEADS - 2:
                                pe.wait_ge(xT_lo_done["b"], TB + 2)
                        pad = slice(1, 3) if h % 2 == 0 else slice(0, 2)
                        last = product(HEAD_OUT[(h // 2) % 2][:, :],
                                       [((vp_hi[:, j, pad].rearrange("p a d -> p (a d)"),
                                          vp_lo[:, j, pad].rearrange("p a d -> p (a d)")),
                                         (probT_hi[:, h % 2, j, :], probT_lo[:, h % 2, j, :]))],
                                       start=h % 2 == 0 and j == 0, stop=h % 2 == 1 and j == TB - 1)
                        if j == TB - 1:
                            last.then_inc(pv_done, 1)
                    if 0 <= u - TURN_LAG < UNITS:
                        w = v - TURN_LAG
                        pe.wait_ge(prob_done, w + 1)
                        if w >= 2:
                            pe.wait_ge(probT_lo_done, w - 1)
                        turn(TURN[w % 2], prob[:, w % SLOTS, :]).then_inc(prob_turned, 1)
                    t = tile_at(u, TURN_AT[b], TURN_EVERY[b])
                    if t is not None:
                        if t == 0:
                            pe.wait_ge(proj_lo_done, LOS * (b + 1))
                        if (b, t) == (0, 1):
                            pe.wait_ge(oT_lo_done, 2)
                        if (b, t) == (0, TB - 1):
                            pe.wait_ge(exp_done, UNITS - 2)
                        if b == 0 and t >= 2:
                            pe.wait_ge(xT_lo_done["b"], TB + t - 1)
                        if (b, t) == (1, 0):
                            pe.wait_ge(exp_done, B * UNITS)
                        if (b, t) == (1, 2):
                            pe.wait_ge(oT_lo_done, B * PAIRS - 1)
                        if (b, t) == (1, TB - 1):
                            pe.wait_ge(xT_lo_done["c"], 1)
                        xn_turn("bc"[b], (TB, 0)[b] + t, NORM_BANKS[b])
                    for p in q_at(u):
                        q_pair(b, p)
                    if b == 0 and u == KV_AT:
                        k_and_v(1)
                    if b == 0 and u == KV_AT + 2:
                        v_turn(1)
                if b == 0:
                    q_pair(1, 0)
                y_begin(b)
                y_end(b)

            def hidden(e, n, slot, s, first):
                v = 2 * NF * e + n
                if not (first and n < 2):
                    pe.wait_ge(act_done, v - 1)
                for kind, bank_of, done in ((0, GATE, gate_done), (1, UP, up_done)):
                    product(bank_of[n % 2][:, :],
                            [((guT_hi[:, slot, kind, j, :], guT_lo[:, slot, kind, j, :]), xT_cols(j, s * S, S))
                             for j in range(KD)]).then_inc(done, 1)

            def expert(e, first, last):
                for n, (c, s) in enumerate(hidden_order(first)):
                    if first:
                        if n == 0:
                            pe.wait_ge(xT_lo_done["c"], TB)
                        if n == NORM_TURN:
                            pe.wait_ge(y_copied, NT)
                            for t in range(TB, NT):
                                xn_turn("c", t, Y_OF[1])
                        if n == LOGITS_AT:
                            pe.wait_ge(xT_lo_done["c"], NT)
                            pe.wait_ge(rw_lo_done, 1)
                            for half in range(2):
                                for j in range(KD):
                                    both = rw[:, j].rearrange("p r e -> p (r e)")
                                    x_hi, x_lo = xT_cols(j, half * S, S)
                                    nc.tensor.matmul(TURN[half][0:2 * E, :], both, x_lo, start=(j == 0), stop=False)
                                    last = nc.tensor.matmul(TURN[half][0:2 * E, :], both, x_hi, start=False, stop=(j == KD - 1))
                                last.then_inc(logits_done, 1)
                        if n == LOGITS_AT + 1:
                            pe.wait_ge(logits_copied, 2)
                            for t in range(NT):
                                last = nc.tensor.transpose(TURN[0][:, 2 * E * t:2 * E * (t + 1)], logitT[:, tile_cols(t)],
                                                           ident[0:2 * E, 0:2 * E])
                            last.then_inc(logits_turned, 1)
                        pe.wait_ge(guT_lo_done, n + 1)
                    elif n % 2 == 0:
                        pe.wait_ge(guT_lo_done, NF * e + (NF + c + 1))
                    slot = n % 2 if first else c % 2
                    hidden(e, n, slot, s, first)
                for t in range(NT):
                    if t == 0:
                        pe.wait_ge(dnT_lo_done, NF * e + NF)
                        pe.wait_ge(hT_lo_done, NF if first else 2 * (NF * e + NF) - 1)
                    if t == TB:
                        pe.wait_ge(hT_lo_done, 2 * (NF * e + NF))
                    if not (first and t < 2):
                        pe.wait_ge(combined, NT * e + (t - 1))
                    product(DOWN_OUT[t % 2][:, :],
                            [((hT_hi[:, c, tile_cols(t)], hT_lo[:, c, tile_cols(t)]), (dnT_hi[:, c, :], dnT_lo[:, c, :]))
                             for c in range(NF)]).then_inc(down_done, 1)

            expert(0, True, False)
            with pe.Fori(1, E - 1) as e:
                expert(e, False, False)
            expert(E - 1, False, True)


def kernel(**inputs):
    import numpy as _np
    import concourse.bacc as _bacc
    from concourse import mybir as _mybir
    from concourse.bass_utils import run_bass_kernel_spmd as _run

    given = {k.replace("L0_attn_", "").replace("L0_ffn_", ""): v for k, v in inputs.items()}
    ctx = given["ctx_1024"]
    b, length, d = ctx.shape
    e, f, _ = given["w_gate"].shape
    laid = {
        "x": given["x"],
        "ctx_rows": ctx,
        "ctx_turned": ctx.reshape(b * length // 256, 256, d // 128, 128).transpose(0, 3, 2, 1),
        "Wq": given["Wq"], "Wkv": given["Wkv"], "Wo": given["Wo"],
        "norm_w": given["norm_w"], "norm_b": given["norm_b"],
        "out_norm_w": given["out_norm_w"], "out_norm_b": given["out_norm_b"],
        "router_turned": given["router_w"].T,
        "gate_up": _np.stack([given["w_gate"].reshape(e, f // 128, 128, d // 128, 128),
                              given["w_up"].reshape(e, f // 128, 128, d // 128, 128)]).transpose(1, 2, 5, 0, 4, 3),
        "down": given["w_down"].reshape(e, d, f // 256, 2, 128).transpose(0, 2, 4, 3, 1),
    }
    nc = _bacc.Bacc("TRN2", target_bir_lowering=False, num_devices=1)
    arrays, args = {}, []
    for name, a in laid.items():
        a = _np.ascontiguousarray(a)
        arrays[f"in_{name}"] = a
        args.append(nc.dram_tensor(f"in_{name}", a.shape, _mybir.dt.from_np(a.dtype), kind="ExternalInput").ap())
    out = nc.dram_tensor("out_x", given["x"].shape, F32, kind="ExternalOutput").ap()
    build(nc, *args, out)
    r = _run(nc, [arrays], core_ids=[0])
    return r.results[0]["out_x"]
```
